# Optimizing a Trainium2 kernel written in Bass

```python
import numpy as np
import jax
import jax.numpy as jnp

def _softmax(x, axis=-1):
    return jax.nn.softmax(x, axis=axis)

def _gelu(x):
    return jax.nn.gelu(x, approximate=True)

def _silu(x):
    return jax.nn.silu(x)

def _sigmoid(x):
    return jax.nn.sigmoid(x)

def _layernorm(x, axis=-1, eps=1e-05):
    m = jnp.mean(x, axis=axis, keepdims=True)
    v = jnp.var(x, axis=axis, keepdims=True)
    return (x - m) / jnp.sqrt(v + eps)

def _scatter_add(tgt, idx, src, axis=0):
    return tgt.at[idx].add(src)

def _segment_sum(src, seg, n):
    return jax.ops.segment_sum(src, seg, n)
kernel_name = 'mk_adaln_d1_jaxref_r4_b3b721'

def setup_inputs(seed: int=0):
    np.random.seed(seed)
    _w = jnp.asarray

    def _L0_attn_setup():
        import jax, jax.numpy as jnp
        import numpy as np
        NUM_HEADS = 16
        NEG = -1000000000.0

        def _split_heads(t, h):
            *lead, s, hd = t.shape
            return jnp.swapaxes(t.reshape(*lead, s, h, hd // h), -3, -2)
        key = jax.random.key(seed)
        ks = jax.random.split(key, 5)
        B, S, D = (4, 512, 256)
        scale = 1.0 / np.sqrt(D)
        return {'x': jax.random.normal(ks[0], (B, S, D), dtype=jnp.float32), 'WQ': jax.random.normal(ks[1], (D, D), dtype=jnp.float32) * scale, 'WK': jax.random.normal(ks[2], (D, D), dtype=jnp.float32) * scale, 'WV': jax.random.normal(ks[3], (D, D), dtype=jnp.float32) * scale, 'WO': jax.random.normal(ks[4], (D, D), dtype=jnp.float32) * scale}
    _L0_attn_in = _L0_attn_setup()

    def _L0_ffn_setup():
        import jax, jax.numpy as jnp
        import numpy as np
        NUM_GEMMS = 8
        HIDDEN = 256
        INTER = 1024
        key = jax.random.key(seed)
        k_x, k_w1, k_b1, k_w2, k_b2 = jax.random.split(key, 5)
        x = jax.random.normal(k_x, (8, 512, HIDDEN), dtype=jnp.float32)
        s1 = 1.0 / np.sqrt(HIDDEN)
        s2 = 1.0 / np.sqrt(INTER)
        W1 = jax.random.uniform(k_w1, (NUM_GEMMS, INTER, HIDDEN), jnp.float32, -s1, s1)
        b1 = jax.random.uniform(k_b1, (NUM_GEMMS, INTER), jnp.float32, -s1, s1)
        W2 = jax.random.uniform(k_w2, (NUM_GEMMS, HIDDEN, INTER), jnp.float32, -s2, s2)
        b2 = jax.random.uniform(k_b2, (NUM_GEMMS, HIDDEN), jnp.float32, -s2, s2)
        return {'x': x, 'W1': W1, 'b1': b1, 'W2': W2, 'b2': b2}
    _L0_ffn_in = _L0_ffn_setup()
    _L0_c = _w((lambda *s: np.random.randn(*s).astype(np.float32) * 0.05)(16, 256))
    _L0_wmod = _w((lambda *s: np.random.randn(*s).astype(np.float32) * 0.05)(256, 6 * 256) * 256 ** (-0.5))
    _d = {'L0_attn_x': _L0_attn_in['x'], 'L0_attn_WQ': _L0_attn_in['WQ'], 'L0_attn_WK': _L0_attn_in['WK'], 'L0_attn_WV': _L0_attn_in['WV'], 'L0_attn_WO': _L0_attn_in['WO'], 'L0_ffn_W1': _L0_ffn_in['W1'], 'L0_ffn_b1': _L0_ffn_in['b1'], 'L0_ffn_W2': _L0_ffn_in['W2'], 'L0_ffn_b2': _L0_ffn_in['b2'], 'L0_c': _L0_c, 'L0_wmod': _L0_wmod}
    _x0 = _d['L0_attn_x']
    _d['L0_attn_x'] = jax.random.normal(jax.random.fold_in(jax.random.key(seed), 1), (16, 1024, 256), dtype=_x0.dtype)
    del _x0
    return _d

def reference(L0_attn_x, L0_attn_WQ, L0_attn_WK, L0_attn_WV, L0_attn_WO, L0_ffn_W1, L0_ffn_b1, L0_ffn_W2, L0_ffn_b2, L0_c, L0_wmod):

    def _L0_attn_ref(x, WQ, WK, WV, WO):
        import jax, jax.numpy as jnp
        import numpy as np
        NUM_HEADS = 16
        NEG = -1000000000.0

        def _split_heads(t, h):
            *lead, s, hd = t.shape
            return jnp.swapaxes(t.reshape(*lead, s, h, hd // h), -3, -2)
        h = NUM_HEADS
        S = x.shape[-2]
        Q = _split_heads(x @ WQ.T, h)
        K = _split_heads(x @ WK.T, h)
        V = _split_heads(x @ WV.T, h)
        dk = Q.shape[-1]
        scores = jnp.einsum('bhqd,bhkd->bhqk', Q, K) / jnp.sqrt(jnp.float32(dk))
        causal = jnp.tril(jnp.ones((S, S), dtype=bool))
        scores = jnp.where(causal, scores, NEG)
        m = jnp.max(scores, axis=-1, keepdims=True)
        e = jnp.exp(scores - m)
        attn = e / jnp.sum(e, axis=-1, keepdims=True)
        out = jnp.einsum('bhqk,bhkd->bhqd', attn, V)
        out = jnp.swapaxes(out, -3, -2).reshape(*x.shape[:-1], -1)
        return out @ WO.T

    def _L0_ffn_ref(x, W1, b1, W2, b2):
        import jax, jax.numpy as jnp
        import numpy as np
        NUM_GEMMS = 8
        HIDDEN = 256
        INTER = 1024
        orig_shape = x.shape
        token_num = int(np.prod(orig_shape[:-1]))
        m = token_num // NUM_GEMMS
        xg = x.reshape(NUM_GEMMS, m, HIDDEN)
        h1 = jnp.einsum('gmh,goh->gmo', xg, W1) + b1[:, None, :]
        h2 = jnp.einsum('gmo,gho->gmh', h1, W2) + b2[:, None, :]
        return h2.reshape(orig_shape)
    x = L0_attn_x
    mod = (_silu(L0_c) @ L0_wmod).reshape(L0_c.shape[0], 6, 1, -1)
    sa, ca, ga, sb, cb, gb = (mod[:, 0], mod[:, 1], mod[:, 2], mod[:, 3], mod[:, 4], mod[:, 5])
    ga = (2 * (ga >= 0) - 1) * jnp.maximum(jnp.abs(ga), 0.25)
    gb = (2 * (gb >= 0) - 1) * jnp.maximum(jnp.abs(gb), 0.25)
    h = _layernorm(x, axis=-1) * (1 + ca) + sa
    x = x + ga * _L0_attn_ref(h, L0_attn_WQ, L0_attn_WK, L0_attn_WV, L0_attn_WO)
    h = _layernorm(x, axis=-1) * (1 + cb) + sb
    x = x + gb * _L0_ffn_ref(h, L0_ffn_W1, L0_ffn_b1, L0_ffn_W2, L0_ffn_b2)
    return x

_drawn_inputs = setup_inputs


def setup_inputs(seed=0):
    import zlib

    import numpy as np

    out = dict(_drawn_inputs(seed))
    spreads = {}
    factors = {'L0_ffn_b1': 8.0, 'L0_ffn_b2': 8.0}
    for name, (base, spread) in spreads.items():
        noise = np.random.default_rng([zlib.crc32(name.encode()), seed]).standard_normal(out[name].shape)
        drawn = base * np.exp(spread * noise) if base else spread * noise
        out[name] = jnp.asarray(drawn.astype(out[name].dtype))
    for name, factor in factors.items():
        out[name] = (out[name] * factor).astype(out[name].dtype)
    return out
```

```python
from contextlib import ExitStack

import concourse.bass as bass
from concourse import mybir

F32 = mybir.dt.float32
BF16 = mybir.dt.bfloat16
ALU = mybir.AluOpType
ACT = mybir.ActivationFunctionType
AX_X = mybir.AxisListType.X

P = 128
STEPS = 48
UNIT = 12
AHEAD = 18
LAG = 2
RING = 4

QK_AT = [0, 2, 3, 5, 8, 12, 20, 22]
WO_AT = [14, 15, 16, 17]
CT_AT = [23, 24, 25, 26]
FF_AT = [27, 28, 29, 30]
V_AT = [32, 36, 37, 38]
AT_AT = [42, 44, 45, 46]
MT_AT = [7, 19, 31, 43]
STATS_A_AT = [31, 32, 33, 35]


def exp_step(k):
    c, j = (0, k) if k < 4 else (1, k - 4)
    diagonal = j >= 4 * c
    width = 512 - 128 * (j - 4 * c) if diagonal else 512
    return c, j, width, diagonal


def max_step(k):
    if k < 4:
        return k, 0, 128 * (k + 1), True
    t, half = 4 + (k - 4) // 2, (k - 4) % 2
    return t, half, (128 * (t - 3) if half else 512), half == 1


def masks_before(k):
    return sum(exp_step(i)[3] for i in range(k + 1))


def adaln_block(nc, x, wq, wk, wv, wo, w1, b1, w2, b2, cT, wmod, out):
    B, S, D = x.shape
    G, O = w1.shape[0], w1.shape[1]
    NT = S // P
    DH = D // P
    KT = O // P
    EPS = 1e-5
    assert (S, D, NT, DH, KT) == (1024, 256, 8, 2, 8) and B == 2 * G

    qk_dram = nc.dram_tensor("qk_parts", [B, 2, 3, D, S], BF16, kind="Internal").ap()
    nmax_dram = nc.dram_tensor("nmax_parts", [B, 4, 3, 32, P], BF16, kind="Internal").ap()
    den_dram = nc.dram_tensor("denominators", [B, 4, 4, S], F32, kind="Internal").ap()
    rden_dram = nc.dram_tensor("reciprocals", [B, 4, 4, S], F32, kind="Internal").ap()
    gate_dram = nc.dram_tensor("gates", [B, 3 * D], F32, kind="Internal").ap()
    ff_dram = nc.dram_tensor("ff_product", [B, P, DH, D], F32, kind="Internal").ap()

    with ExitStack() as ctx:
        def sb(name, shape, dt=F32):
            return ctx.enter_context(nc.sbuf_tensor(name, shape, dt))

        def ps(name, shape):
            return ctx.enter_context(nc.psum_tensor(name, shape, F32))

        def sem(name):
            return ctx.enter_context(nc.semaphore(name))

        q_stack = sb("q_stack", [P, RING, 4, S], BF16)
        k_stack = sb("k_stack", [P, RING, 4, S], BF16)
        probs = sb("probs", [P, RING, 4, 512])
        xn = sb("xn", [P, NT, D])
        xres = sb("xres", [P, NT, D])
        hT_a = sb("hT_a", [P, DH, S])
        hT_c = sb("hT_c", [P, DH, S])
        v_row = sb("v_row", [P, NT, D])
        v_ones = sb("v_ones", [P, 2, NT, 4, 32])
        o_both = sb("o_both", [P, 2, DH, S])
        o_num, o_rden = o_both[:, 0], o_both[:, 1]
        den_cols = sb("den_cols", [P, 2, 32])
        o_raw = sb("o_raw", [P, 2, S])
        parts = sb("parts", [P, 4, 3, 512], BF16)
        rest = sb("rest", [P, 2, 512])
        wq_sb, wk_sb, wv_sb, wo_sb = (sb(n, [P, DH, D]) for n in ("wq_sb", "wk_sb", "wv_sb", "wo_sb"))
        wo_gated = sb("wo_gated", [P, DH, D])
        ff_gated = sb("ff_gated", [P, DH, D])
        gates = sb("gates_sb", [P, 3 * D])
        causal = sb("causal", [P, 512])
        ident = sb("ident", [P, P])
        scratch = sb("scratch", [P, 2, 512], BF16)
        mod_cols = sb("mod_cols", [P, B, 4, DH])
        mod_a = sb("mod_a", [P, 4, DH])
        mod_c = sb("mod_c", [P, 4, DH])
        exponent = sb("exponent", [P, NT])
        stats = sb("stats", [P, 2, NT, 6])
        mean_var = sb("mean_var", [P, 2, NT, 2])
        rstd = sb("rstd", [P, 2, NT])
        mx = sb("mx", [P, 2, 4, NT])
        mx_low = sb("mx_low", [P, 2, 4, 4])
        nmax = sb("nmax", [32, 3, P], BF16)
        nrest = sb("nrest", [32, P])
        c_sb = sb("c_sb", [P, DH, B])
        c_exp = sb("c_exp", [P, DH, B])
        b1_sb = sb("b1_sb", [P, G, KT])

        wmod_sb = o_both[:, :, :, :].rearrange("p a h s -> p (a h s)")[:, 0:DH * 6 * D].rearrange(
            "p (h n) -> p h n", h=DH)
        w12 = probs[:, :, :, :].rearrange("p r h q -> p (r h q)").rearrange(
            "p (s m k n) -> p s m k n", s=2, m=2, k=KT)
        ff_out = hT_c[:, 0, :].rearrange("p (s h n) -> p s h n", s=2, h=DH)
        bias_row = hT_c[0:1, 1, 0:2 * D].rearrange("p (s n) -> p s n", s=2)
        g_pos, g_neg = o_raw[0:B, 0, 0:2 * D], o_raw[0:B, 1, 0:2 * D]
        b2_sb = xres[0:1, :, :]

        ps_max = ps("ps_max", [P, 2, 512])
        ps_exp = ps("ps_exp", [P, 4, 512])
        ps_out = ps("ps_out", [P, 512])
        ps_misc = ps("ps_misc", [P, 512])

        mod_loaded, x0_weights_loaded, b_loaded = sem("mod_loaded"), sem("weights_loaded"), sem("b_loaded")
        x_loaded, c_loaded, w12_loaded = sem("x_loaded"), sem("c_loaded"), [sem("w12_loaded0"), sem("w12_loaded1")]
        consts_ready, const_step, ones_ready = sem("consts_ready"), sem("const_step"), sem("ones_ready")
        cexp_done, silu_step, mod_ps, mod_ev, gate_step, gate_stored = (
            sem(n) for n in ("cexp_done", "silu_step", "mod_ps", "mod_ev", "gate_step", "gate_stored"))
        w12_ps, w12_ev, bias_ev = (sem(n) for n in ("w12_ps", "w12_ev", "bias_ev"))
        w12_stored = [sem("w12_stored0"), sem("w12_stored1")]
        a_rstd, c_rstd = sem("a_rstd"), sem("c_rstd")
        a_step, a_normed, aT_ps, aT_ev = (sem(n) for n in ("a_step", "a_normed", "aT_ps", "aT_ev"))
        qk_ps, qk_hi, qk_copied, qk_rest, qk_mid, qk_low = (
            sem(n) for n in ("qk_ps", "qk_hi", "qk_copied", "qk_rest", "qk_mid", "qk_low"))
        qk_stored = [sem(f"qk_stored{i}") for i in range(4)]
        stack_loaded = [sem(f"stack_loaded{i}") for i in range(RING)]
        v_ps, v_ev, v_copied = sem("v_ps"), sem("v_ev"), sem("v_copied")
        smax_ps, smax_done, mx_joined, mT_ps, nmax_step, nmax_stored, nmax_loaded = (
            sem(n) for n in ("smax_ps", "smax_done", "mx_joined", "mT_ps", "nmax_step", "nmax_stored", "nmax_loaded"))
        sexp_ps, exp_done, masked, pv_done, o_copied = (
            sem(n) for n in ("sexp_ps", "exp_done", "masked", "pv_done", "o_copied"))
        num_moved, rden_spread = ([sem(f"{n}{i}") for i in range(2)] for n in ("num_moved", "rden_spread"))
        den_stored, den_loaded, inverted, rden_stored = (
            sem(n) for n in ("den_stored", "den_loaded", "inverted", "rden_stored"))
        gated, divided, wo_ps, x1_done, c_step, c_normed, cT_ps, cT_ev, biased, ff_ps, ff_done, out_stored = (
            sem(n) for n in ("gated", "divided", "wo_ps", "x1_done", "c_step", "c_normed", "cT_ps", "cT_ev",
                             "biased", "ff_ps", "ff_done", "out_stored"))

        waits_met = sem("waits_met")

        def stand_alone(eng):
            eng.sem_inc(waits_met, 1)

        def any_yet(count):
            return not isinstance(count, int) or count > 0

        block = ctx.enter_context(nc.Block())

        @block.sync
        def _(sp):
            def load_stack(b, g):
                for s in range(4):
                    if any_yet(32 * b + (16 if g < 2 else 32)):
                        sp.wait_ge(qk_stored[s], 32 * b + (16 if g < 2 else 32))
                        stand_alone(sp)
                if any_yet(96 * b - 96 + 24 * (g + 1)):
                    sp.wait_ge(sexp_ps, 96 * b - 96 + 24 * (g + 1))
                    stand_alone(sp)
                for r, (qp, kp) in enumerate([(0, 0), (0, 1), (0, 2), (1, 0), (1, 1), (2, 0)]):
                    for stack, m, part in ((q_stack, 0, qp), (k_stack, 1, kp)):
                        sp.dma_start(
                            stack[16 * r:16 * r + 16, g, :, :],
                            qk_dram[b, m, part, 64 * g:64 * g + 64, :].rearrange("(h d) s -> d h s", d=16),
                        ).then_inc(stack_loaded[g], 16)

            def move_maxima(b, g):
                u = 4 * b + g
                sp.wait_ge(nmax_step, 4 * u + 4)
                stand_alone(sp)
                sp.dma_start(nmax_dram[b, g].rearrange("t r q -> r t q"), nmax[:, :, :]).then_inc(nmax_stored, 16)
                sp.wait_ge(nmax_stored, 16 * u + 16)
                stand_alone(sp)
                if any_yet(24 * u - 72):
                    sp.wait_ge(sexp_ps, 24 * u - 72)
                    stand_alone(sp)
                sp.dma_start(
                    q_stack[96:99, g, :, :].rearrange("p h s -> p (h s)"),
                    nmax_dram[b, g].rearrange("t r q -> t (r q)"),
                ).then_inc(nmax_loaded, 16)

            def store_parts(b, i):
                m, oh, half = (i // 2) % 2, i // 4, i % 2
                sp.wait_ge(qk_low, 8 * b + i + 1)
                stand_alone(sp)
                sp.dma_start(
                    qk_dram[b, m, :, P * oh:P * oh + P, 512 * half:512 * half + 512].rearrange("t p s -> p t s"),
                    parts[:, i % 4, :, :],
                ).then_inc(qk_stored[i % 4], 16)

            def move_output(b, g):
                u = 4 * b + g
                sp.wait_ge(o_copied, 2 * u + 2)
                stand_alone(sp)
                sp.dma_start(den_dram[b, g], o_raw[16:P:32, g % 2, :]).then_inc(den_stored, 16)
                if any_yet(4 * b):
                    sp.wait_ge(wo_ps, 4 * b)
                    stand_alone(sp)
                for h in range(4):
                    at = 64 * (g % 2) + 16 * h
                    sp.dma_start(o_num[at:at + 16, g // 2, :], o_raw[32 * h:32 * h + 16, g % 2, :]
                                 ).then_inc(num_moved[g % 2], 16)
                sp.wait_ge(den_stored, 16 * u + 16)
                stand_alone(sp)
                sp.dma_start(den_cols[:, g % 2, :], den_dram[b, g].rearrange("h (p c) -> (h p) c", c=32)
                             ).then_inc(den_loaded, 16)

            def spread_reciprocals(b, g):
                u = 4 * b + g
                sp.wait_ge(inverted, u + 1)
                stand_alone(sp)
                sp.dma_start(rden_dram[b, g].rearrange("h (p c) -> (h p) c", c=32), den_cols[:, g % 2, :]
                             ).then_inc(rden_stored, 16)
                if any_yet(2 * b):
                    sp.wait_ge(divided, 2 * b)
                    stand_alone(sp)
                sp.wait_ge(rden_stored, 16 * u + 16)
                stand_alone(sp)
                for h in range(4):
                    at = 64 * (g % 2) + 16 * h
                    sp.dma_start(o_rden[at:at + 16, g // 2, :], rden_dram[b, g, h].partition_broadcast(16)
                                 ).then_inc(rden_spread[g % 2], 16)

            def load_x(b):
                if any_yet(4 * b):
                    sp.wait_ge(aT_ps, 4 * b)
                    stand_alone(sp)
                if any_yet(4 * b - 8):
                    sp.wait_ge(cT_ps, 4 * b - 8)
                    stand_alone(sp)
                sp.dma_start(xn[:, :, :], x[b].rearrange("(t p) d -> p t d", p=P)).then_inc(x_loaded, 16)

            def load_c(b):
                if any_yet(4 * b):
                    sp.wait_ge(gated, 4 * b)
                    stand_alone(sp)
                if any_yet(8 * b):
                    sp.wait_ge(biased, 8 * b)
                    stand_alone(sp)
                sp.dma_start(gates[:, :], gate_dram[b].partition_broadcast(P)).then_inc(c_loaded, 16)
                if any_yet(4 * b):
                    sp.wait_ge(ff_ps, 4 * b)
                    stand_alone(sp)
                sp.dma_start(ff_gated[:, :, :], ff_dram[b]).then_inc(c_loaded, 16)
                if any_yet(16 * b):
                    sp.wait_ge(out_stored, 16 * b)
                    stand_alone(sp)
                sp.dma_start(xres[:, :, :], x[b].rearrange("(t p) d -> p t d", p=P)).then_inc(c_loaded, 16)

            def store_out(b):
                sp.wait_ge(ff_done, 4 * b + 4)
                stand_alone(sp)
                sp.dma_start(out[b].rearrange("(t p) d -> p t d", p=P), xres[:, :, :]).then_inc(out_stored, 16)

            def row(b, first, last, two_more):
                for n in range(STEPS):
                    if n == 28 and two_more:
                        load_x(b + 2)
                    if n == 0:
                        if not first:
                            load_c(b - 1)
                            load_stack(b, 3)
                    if n == 2 and not first:
                        move_output(b - 1, 3)
                    if n - 2 in MT_AT:
                        g = MT_AT.index(n - 2) + 1
                        if g < 4 or not last:
                            move_maxima(b + g // 4, g % 4)
                    if n in (19, 31, 43):
                        move_output(b, n // UNIT - 1)
                    if n in (21, 33, 45):
                        spread_reciprocals(b, n // UNIT - 1)
                    if n == 4 and not first:
                        spread_reciprocals(b - 1, 3)
                    if n - 3 in QK_AT and not last:
                        store_parts(b + 1, QK_AT.index(n - 3))
                    if n in (18, 27, 38) and not last:
                        load_stack(b + 1, (18, 27, 38).index(n))
                    if n == 33 and not first:
                        store_out(b - 1)

            sp.dma_start(c_sb[:, :, :], cT.rearrange("(h p) b -> p h b", p=P)).then_inc(mod_loaded, 16)
            load_x(0)
            sp.dma_start(wmod_sb, wmod.rearrange("(h p) n -> p h n", p=P)).then_inc(mod_loaded, 16)
            for buf, w in ((wq_sb, wq), (wk_sb, wk), (wv_sb, wv), (wo_sb, wo)):
                sp.dma_start(buf[:, :, :], w.rearrange("(h p) n -> p h n", p=P)).then_inc(x0_weights_loaded, 16)
            sp.dma_start(b1_sb[:, :, :], b1).then_inc(b_loaded, 16)
            sp.dma_start(b2_sb, b2.rearrange("(a g) n -> a g n", a=1)).then_inc(b_loaded, 16)
            sp.wait_ge(gate_step, 5)
            stand_alone(sp)
            sp.dma_start(gate_dram[:, 0:2 * D], g_pos).then_inc(gate_stored, 16)
            for i in range(4):
                store_parts(0, i)
            load_stack(0, 0)
            load_stack(0, 1)
            for i in range(4, 8):
                store_parts(0, i)
            load_stack(0, 2)
            load_stack(0, 3)
            load_x(1)
            move_maxima(0, 0)
            sp.wait_ge(mod_ps, 10)
            stand_alone(sp)
            sp.wait_ge(gate_stored, 16)
            stand_alone(sp)
            for s in range(2):
                sp.wait_ge(w12_stored[s], 64 * (G // 2))
                stand_alone(sp)
            row(0, True, False, True)
            with sp.Fori(1, B - 2) as b:
                row(b, False, False, True)
            row(B - 2, False, False, False)
            row(B - 1, False, True, False)
            load_c(B - 1)
            move_output(B - 1, 3)
            spread_reciprocals(B - 1, 3)
            store_out(B - 1)
            sp.wait_ge(out_stored, 16 * B)
            stand_alone(sp)
            for s in range(4):
                sp.wait_ge(qk_stored[s], 32 * B)
                stand_alone(sp)
            for s in (nmax_stored, den_stored, rden_stored):
                sp.wait_ge(s, 64 * B)
                stand_alone(sp)

        @block.tensor
        def _(pe):
            copied, count = mod_ev, 1

            def misc_copied_by(s, value):
                nonlocal copied, count
                copied, count = s, value

            def scores_for_max(b, n, h):
                g, k = divmod(n + AHEAD, UNIT)
                t, half, width, _ = max_step(k)
                if k == 0 and h == 0:
                    pe.wait_ge(stack_loaded[g % 4], 192 * (b + g // 4) + 192)
                at = 4 * STEPS * b + 4 * (n + AHEAD) + h
                if any_yet(at - 1):
                    pe.wait_ge(smax_done, at - 1)
                nc.tensor.matmul(ps_max[:, h % 2, 0:width], q_stack[0:96, g % 4, h, P * t:P * t + P],
                                 k_stack[0:96, g % 4, h, 512 * half:512 * half + width],
                                 start=True, stop=True).then_inc(smax_ps, 1)

            def scores_for_exp(b, n, pair):
                g, k = divmod(n, UNIT)
                c, j, width, _ = exp_step(k)
                if k == 0 and pair == 0:
                    pe.wait_ge(nmax_loaded, 64 * b + 16 * g + 16)
                if any_yet(96 * b + 2 * n + pair - 1):
                    pe.wait_ge(exp_done, 96 * b + 2 * n + pair - 1)
                for h in (2 * pair, 2 * pair + 1):
                    q0 = 512 * c + 512 - width
                    last = nc.tensor.matmul(ps_exp[:, h, 0:width], k_stack[0:99, g, h, P * j:P * j + P],
                                            q_stack[0:99, g, h, q0:q0 + width], start=True, stop=True)
                last.then_inc(sexp_ps, 1)

            def values(b, n):
                g, k = divmod(n, UNIT)
                c, j, width, diagonal = exp_step(k)
                pe.wait_ge(exp_done, 96 * b + 2 * n + 2)
                if diagonal:
                    if any_yet(32 * b + 8 * g + masks_before(k)):
                        pe.wait_ge(masked, 32 * b + 8 * g + masks_before(k))
                if k == 0:
                    pe.wait_ge(v_copied, 4 * b + g + 1)
                if j == 0:
                    if any_yet(8 * b + 2 * g + c):
                        pe.wait_ge(o_copied, 8 * b + 2 * g + c)
                for h in range(4):
                    last = nc.tensor.matmul(ps_out[32 * h:32 * h + 32, 512 - width:512],
                                            v_ones[:, g % 2, j, h, :], probs[:, n % RING, h, 0:width],
                                            start=(j == 0), stop=(k in (3, 11)))
                last.then_inc(pv_done, 1)

            def transpose_normed(b, i, normed, ps_sem, ev_sem):
                half, dh = divmod(i, 2)
                pe.wait_ge(normed, 4 * b + 2 * half + 2)
                pe.wait_ge(copied, count)
                misc_copied_by(ev_sem, 4 * b + i + 1)
                for t in range(4):
                    last = nc.tensor.transpose(ps_misc[:, P * t:P * t + P],
                                               xn[:, 4 * half + t, P * dh:P * dh + P], ident[:, :])
                last.then_inc(ps_sem, 1)

            def project_qk(b, i):
                m, oh, half = (i // 2) % 2, i // 4, i % 2
                pe.wait_ge(aT_ev, 4 * b + 2 * half + 2)
                pe.wait_ge(copied, count)
                misc_copied_by(qk_copied, 8 * b + i + 1)
                w = wk_sb if m else wq_sb
                for dh in range(DH):
                    last = nc.tensor.matmul(ps_misc[:, :], w[:, dh, P * oh:P * oh + P],
                                            hT_a[:, dh, 512 * half:512 * half + 512],
                                            start=(dh == 0), stop=(dh == DH - 1))
                last.then_inc(qk_ps, 1)

            def by_token(i, hT, w, rows):
                for t in range(2):
                    for dh in range(DH):
                        last = nc.tensor.matmul(ps_misc[:, D * t:D * t + D],
                                                hT[:, dh, P * (2 * i + t):P * (2 * i + t) + P], w[:, dh, :],
                                                start=(dh == 0), stop=(dh == DH - 1))
                last.then_inc(rows, 1)

            def project_v(b, i):
                pe.wait_ge(aT_ev, 4 * b + 4)
                pe.wait_ge(copied, count)
                misc_copied_by(v_ev, 4 * b + i + 1)
                by_token(i, hT_a, wv_sb, v_ps)

            def project_out(b, i):
                pe.wait_ge(divided, 2 * b + 2)
                pe.wait_ge(gated, 4 * b + 2)
                pe.wait_ge(copied, count)
                misc_copied_by(x1_done, 4 * b + i + 1)
                by_token(i, o_num, wo_gated, wo_ps)

            def feed_forward(b, i):
                pe.wait_ge(cT_ev, 4 * b + 4)
                pe.wait_ge(gated, 4 * b + 4)
                pe.wait_ge(copied, count)
                misc_copied_by(ff_done, 4 * b + i + 1)
                by_token(i, hT_c, ff_gated, ff_ps)

            def maxima_to_rows(b, g):
                u = 4 * b + g
                pe.wait_ge(mx_joined, u + 1)
                pe.wait_ge(copied, count)
                misc_copied_by(nmax_step, 4 * u + 2)
                nc.tensor.matmul(ps_misc[0:32, 0:P], mx[:, g % 2, :, :].rearrange("p h t -> p (h t)"), ident[:, :],
                                 start=True, stop=True).then_inc(mT_ps, 1)

            def ff_product(i):
                g, what = divmod(i, 3)
                if any_yet(32 * (g // 2 + 1)):
                    pe.wait_ge(w12_loaded[g % 2], 32 * (g // 2 + 1))
                if any_yet(2 * ((i - 4) // 3) + min((i - 4) % 3 + 1, 2)):
                    pe.wait_ge(w12_ev, 2 * ((i - 4) // 3) + min((i - 4) % 3 + 1, 2))
                if any_yet((i - 4 + 1) // 3):
                    pe.wait_ge(bias_ev, (i - 4 + 1) // 3)
                w1t, w2t = w12[:, g % 2, 0], w12[:, g % 2, 1]
                for kt in range(KT):
                    lhs = w1t[:, kt, P * what:P * what + P] if what < 2 else b1_sb[:, g, kt:kt + 1]
                    dst = ps_exp[0:P if what < 2 else 1, i % 4, 0:D]
                    last = nc.tensor.matmul(dst, lhs, w2t[:, kt, :], start=(kt == 0), stop=(kt == KT - 1))
                last.then_inc(w12_ps, 1)

            def row(b, first, last, two_more):
                if last:
                    misc_copied_by(nmax_step, 16 * b + 2)
                else:
                    misc_copied_by(aT_ev, 4 * b + 8)
                for n in range(STEPS):
                    ahead = (n + AHEAD) // UNIT < 4 or not last
                    if ahead:
                        scores_for_max(b, n, 0)
                    scores_for_exp(b, n, 0)
                    if ahead:
                        scores_for_max(b, n, 1)
                    if n >= LAG:
                        values(b, n - LAG)
                    elif not first:
                        values(b - 1, n - LAG + STEPS)
                    if ahead:
                        scores_for_max(b, n, 2)
                    scores_for_exp(b, n, 1)
                    if ahead:
                        scores_for_max(b, n, 3)
                    if n in MT_AT:
                        g = MT_AT.index(n) + 1
                        if g < 4 or not last:
                            maxima_to_rows(b + g // 4, g % 4)
                    if not first:
                        if n in WO_AT:
                            project_out(b - 1, WO_AT.index(n))
                        if n in CT_AT:
                            transpose_normed(b - 1, CT_AT.index(n), c_normed, cT_ps, cT_ev)
                        if n in FF_AT:
                            feed_forward(b - 1, FF_AT.index(n))
                    if two_more and n in AT_AT:
                        transpose_normed(b + 2, AT_AT.index(n), a_normed, aT_ps, aT_ev)
                    if not last:
                        if n in QK_AT:
                            project_qk(b + 1, QK_AT.index(n))
                        if n in V_AT:
                            project_v(b + 1, V_AT.index(n))

            pe.wait_ge(mod_loaded, 32)
            pe.wait_ge(silu_step, 3)
            for i, which in enumerate((0, 1, 3, 4)):
                for oh in range(DH):
                    at = B * (DH * i + oh)
                    for dh in range(DH):
                        last = nc.tensor.matmul(ps_misc[:, at:at + B],
                                                wmod_sb[:, dh, D * which + P * oh:D * which + P * oh + P],
                                                c_sb[:, dh, :], start=(dh == 0), stop=(dh == DH - 1))
                    last.then_inc(mod_ps, 1)
            for i, which in enumerate((2, 5)):
                for dh in range(DH):
                    last = nc.tensor.matmul(ps_out[0:B, D * i:D * i + D], c_sb[:, dh, :],
                                            wmod_sb[:, dh, D * which:D * which + D],
                                            start=(dh == 0), stop=(dh == DH - 1))
                last.then_inc(mod_ps, 1)
            pe.wait_ge(consts_ready, 2)
            for i in range(4):
                transpose_normed(0, i, a_normed, aT_ps, aT_ev)
            pe.wait_ge(x0_weights_loaded, 64)
            for i in range(8):
                project_qk(0, i)
            for i in range(4):
                project_v(0, i)
            pe.wait_ge(b_loaded, 32)
            for i in range(6):
                ff_product(i)
            for n in range(AHEAD):
                for h in range(4):
                    scores_for_max(0, n - AHEAD, h)
                ff_product(6 + n)
                if n == UNIT + 1:
                    maxima_to_rows(0, 0)
                if n > UNIT + 1:
                    transpose_normed(1, n - UNIT - 2, a_normed, aT_ps, aT_ev)
            pe.wait_ge(w12_ev, 2 * G)
            pe.wait_ge(bias_ev, G)
            pe.wait_ge(gate_step, 5)
            pe.wait_ge(ones_ready, 3)
            row(0, True, False, True)
            with pe.Fori(1, B - 2) as b:
                row(b, False, False, True)
            row(B - 2, False, False, False)
            row(B - 1, False, True, False)
            for n in range(STEPS - LAG, STEPS):
                values(B - 1, n)
            for i in range(4):
                project_out(B - 1, i)
            for i in range(4):
                transpose_normed(B - 1, i, c_normed, cT_ps, cT_ev)
            for i in range(4):
                feed_forward(B - 1, i)

        @block.scalar
        def _(act):
            def exp(b, n, pair):
                width = exp_step(n % UNIT)[2]
                act.wait_ge(sexp_ps, 96 * b + 2 * n + pair + 1)
                if any_yet(48 * b + n - RING + 1):
                    act.wait_ge(pv_done, 48 * b + n - RING + 1)
                nc.scalar.activation(probs[:, n % RING, 2 * pair:2 * pair + 2, 0:width],
                                     ps_exp[:, 2 * pair:2 * pair + 2, 0:width], ACT.Exp,
                                     scale=0.25).then_inc(exp_done, 1)

            def copy_output(b, n):
                g, k = divmod(n, UNIT)
                c = exp_step(k)[0]
                act.wait_ge(pv_done, 48 * b + n + 1)
                if any_yet(128 * b + 64 * (g // 2)):
                    act.wait_ge(num_moved[g % 2], 128 * b + 64 * (g // 2))
                if any_yet(16 * (4 * b + g - 1)):
                    act.wait_ge(den_stored, 16 * (4 * b + g - 1))
                nc.scalar.copy(o_raw[:, g % 2, 512 * c:512 * c + 512], ps_out[:, :]).then_inc(o_copied, 1)

            def modulate(b, i, ps_sem, ev_sem, mod, hT, mod_ready, free, free_at):
                half, dh = divmod(i, 2)
                act.wait_ge(ps_sem, 4 * b + i + 1)
                act.wait_ge(mod_ready, 3 * b + 2)
                for s, value in zip(free, free_at):
                    if any_yet(value):
                        act.wait_ge(s, value)
                nc.scalar.activation(hT[:, dh, 512 * half:512 * half + 512], ps_misc[:, :], ACT.Identity,
                                     scale=mod[:, 1, dh:dh + 1], bias=mod[:, 0, dh:dh + 1]).then_inc(ev_sem, 1)

            def modulate_a(b, i):
                modulate(b, i, aT_ps, aT_ev, mod_a, hT_a, a_step, (v_ps,), (4 * b,))

            def modulate_c(b, i):
                modulate(b, i, cT_ps, cT_ev, mod_c[:, 2:4, :], hT_c, c_step, (ff_ps,), (4 * b,))

            def copy_qk(b, i):
                act.wait_ge(qk_ps, 8 * b + i + 1)
                if any_yet(8 * b + i - 1):
                    act.wait_ge(qk_low, 8 * b + i - 1)
                nc.scalar.copy(rest[:, i % 2, :], ps_misc[:, :]).then_inc(qk_copied, 1)

            def high_part(b, i):
                act.wait_ge(qk_copied, 8 * b + i + 1)
                if any_yet(32 * b + 16 * (i // 4)):
                    act.wait_ge(qk_stored[i % 4], 32 * b + 16 * (i // 4))
                nc.scalar.copy(parts[:, i % 4, 0, :], rest[:, i % 2, :]).then_inc(qk_hi, 1)

            def middle_part(b, i):
                act.wait_ge(qk_rest, 8 * b + i + 1)
                nc.scalar.copy(parts[:, i % 4, 1, :], rest[:, i % 2, :]).then_inc(qk_mid, 1)

            def copy_v(b, i):
                act.wait_ge(v_ps, 4 * b + i + 1)
                if any_yet(4 * b):
                    act.wait_ge(v_copied, 4 * b)
                nc.scalar.copy(v_row[:, 2 * i:2 * i + 2, :],
                               ps_misc[:, :].rearrange("p (t d) -> p t d", t=2)).then_inc(v_ev, 1)

            def row(b, first, last, two_more):
                for n in range(STEPS):
                    if two_more and n - 1 in AT_AT:
                        modulate_a(b + 2, AT_AT.index(n - 1))
                    if not last and n - 1 in QK_AT:
                        copy_qk(b + 1, QK_AT.index(n - 1))
                    if not last and n - 1 in V_AT:
                        copy_v(b + 1, V_AT.index(n - 1))
                    if not first and n - 1 in CT_AT:
                        modulate_c(b - 1, CT_AT.index(n - 1))
                    exp(b, n, 0)
                    if not last:
                        if n - 2 in QK_AT:
                            middle_part(b + 1, QK_AT.index(n - 2))
                        if n - 1 in QK_AT:
                            high_part(b + 1, QK_AT.index(n - 1))
                    if (n - LAG) % UNIT in (3, 11):
                        if n >= LAG:
                            copy_output(b, n - LAG)
                        elif not first:
                            copy_output(b - 1, n - LAG + STEPS)
                    exp(b, n, 1)

            def product_copy(i):
                g, what = divmod(i, 3)
                act.wait_ge(w12_ps, i + 1)
                if any_yet(64 * (g // 2)):
                    act.wait_ge(w12_stored[g % 2], 64 * (g // 2))
                nc.scalar.copy(ff_out[:, g % 2, what, :], ps_exp[:, i % 4, 0:D]).then_inc(w12_ev, 1)

            act.wait_ge(mod_loaded, 32)
            nc.scalar.activation(c_exp[:, :, :], c_sb[:, :, :], ACT.Exp, scale=-1.0).then_inc(cexp_done, 1)
            for i in range(4):
                modulate_a(0, i)
            for i in range(8):
                copy_qk(0, i)
                high_part(0, i)
                middle_part(0, i)
            for i in range(4):
                copy_v(0, i)
            for i in range(3 * G):
                if i % 3 < 2:
                    product_copy(i)
                if i >= 6 + UNIT + 2:
                    modulate_a(1, i - 6 - UNIT - 2)
            act.wait_ge(w12_ps, 3 * G)
            for s in range(2):
                act.wait_ge(w12_stored[s], 64 * (G // 2))
            row(0, True, False, True)
            with act.Fori(1, B - 2) as b:
                row(b, False, False, True)
            row(B - 2, False, False, False)
            row(B - 1, False, True, False)
            copy_output(B - 1, STEPS - 1)
            for i in range(4):
                modulate_c(B - 1, i)

        @block.vector
        def _(dve):
            def row_max(b, n, h):
                g, k = divmod(n + AHEAD, UNIT)
                t, half, width, diagonal = max_step(k)
                if k == 0 and h == 0:
                    if any_yet(4 * b + g - 1):
                        dve.wait_ge(mT_ps, 4 * b + g - 1)
                dve.wait_ge(smax_ps, 4 * STEPS * b + 4 * (n + AHEAD) + h + 1)
                if diagonal:
                    stand_alone(dve)
                    ins = nc.vector.tensor_tensor_reduce(
                        scratch[:, h % 2, 0:width], ps_max[:, h % 2, 0:width], causal[:, 512 - width:512],
                        1.0, -3.0e38, ALU.add, ALU.max, mx[:, g % 2, h, t:t + 1])
                else:
                    ins = nc.vector.tensor_reduce(mx_low[:, g % 2, h, t - 4:t - 3], ps_max[:, h % 2, :],
                                                  AX_X, ALU.max)
                ins.then_inc(smax_done, 1)

            def join_maxima(b, g):
                u = 4 * b + g
                dve.wait_ge(smax_done, 48 * u + 48)
                nc.vector.tensor_tensor(mx[:, g % 2, :, 4:8], mx[:, g % 2, :, 4:8], mx_low[:, g % 2, :, :],
                                        ALU.max).then_inc(mx_joined, 1)

            def split_maxima(b, g, part):
                u = 4 * b + g
                m = ps_misc[0:32, 0:P]
                if part == 0:
                    dve.wait_ge(mT_ps, u + 1)
                    if any_yet(16 * u):
                        dve.wait_ge(nmax_stored, 16 * u)
                    nc.vector.tensor_scalar(nmax[:, 0, :], m, -1.0, None, ALU.mult).then_inc(nmax_step, 1)
                    dve.wait_ge(nmax_step, 4 * u + 1)
                    nc.vector.scalar_tensor_tensor(out=nrest[:, :], in0=m, scalar=-1.0, in1=nmax[:, 0, :],
                                                   op0=ALU.mult, op1=ALU.subtract).then_inc(nmax_step, 1)
                elif part == 1:
                    dve.wait_ge(nmax_step, 4 * u + 2)
                    nc.vector.tensor_copy(nmax[:, 1, :], nrest[:, :]).then_inc(nmax_step, 1)
                else:
                    dve.wait_ge(nmax_step, 4 * u + 3)
                    nc.vector.tensor_tensor(nmax[:, 2, :], nrest[:, :], nmax[:, 1, :],
                                            ALU.subtract).then_inc(nmax_step, 1)

            def norm_stats(s, src, i):
                for t in (2 * i, 2 * i + 1):
                    last = nc.vector.bn_stats(stats[:, s, t, :], src[:, t, :])
                if i == 3:
                    last.then_inc(c_step if s else a_step, 1)

            def norm_mean_var(b, s):
                step, mod = (c_step, mod_c) if s else (a_step, mod_a)
                dve.wait_ge(step, 3 * b + 1)
                if any_yet(4 * b):
                    dve.wait_ge(cT_ev if s else aT_ev, 4 * b)
                stand_alone(dve)
                for t in range(NT):
                    nc.vector.bn_aggr(mean_var[:, s, t, :], stats[:, s, t, :])
                nc.vector.tensor_copy(mod[:, :, :], mod_cols[:, b, :, :]).then_inc(step, 1)

            def norm_add_eps(b, s):
                step = c_step if s else a_step
                dve.wait_ge(step, 3 * b + 2)
                nc.vector.tensor_scalar(rstd[:, s, :], mean_var[:, s, :, 1], EPS, None, ALU.add).then_inc(step, 1)

            def normalise(b, s, src, i):
                dve.wait_ge(c_rstd if s else a_rstd, b + 1)
                for t in (2 * i, 2 * i + 1):
                    last = nc.vector.tensor_scalar(xn[:, t, :], src[:, t, :], mean_var[:, s, t, 0:1],
                                                   rstd[:, s, t:t + 1], ALU.subtract, ALU.mult)
                last.then_inc(c_normed if s else a_normed, 1)

            def invert(b, g):
                u = 4 * b + g
                dve.wait_ge(den_loaded, 16 * u + 16)
                nc.vector.reciprocal(den_cols[:, g % 2, :], den_cols[:, g % 2, :]).then_inc(inverted, 1)

            def divide(b, dh):
                for s in range(2):
                    dve.wait_ge(num_moved[s], 128 * b + 128)
                    dve.wait_ge(rden_spread[s], 128 * b + 128)
                nc.vector.tensor_tensor(o_num[:, dh, :], o_num[:, dh, :], o_rden[:, dh, :],
                                        ALU.mult).then_inc(divided, 1)

            def add_to_residual(ps_sem, at, i, done):
                if any_yet(at):
                    dve.wait_ge(ps_sem, at)
                r = xres[:, 2 * i:2 * i + 2, :]
                nc.vector.tensor_tensor(r, ps_misc[:, :].rearrange("p (t d) -> p t d", t=2), r,
                                        ALU.add).then_inc(done, 1)

            def attention_residual(b, i):
                dve.wait_ge(c_loaded, 48 * b + 48)
                add_to_residual(wo_ps, 4 * b + i + 1, i, x1_done)

            def feed_forward_residual(b, i):
                dve.wait_ge(biased, 8 * b + 2 * i + 2)
                add_to_residual(ff_ps, 4 * b + i + 1, i, ff_done)

            def row(b, first, last, two_more):
                for n in range(STEPS):
                    ahead = (n + AHEAD) // UNIT < 4 or not last
                    if ahead:
                        row_max(b, n, 0)
                        row_max(b, n, 1)
                    if n - 1 in MT_AT and (n - 1 != MT_AT[3] or not last):
                        g = MT_AT.index(n - 1) + 1
                        split_maxima(b + g // 4, g % 4, 0)
                    if not first:
                        if n - 1 in WO_AT:
                            attention_residual(b - 1, WO_AT.index(n - 1))
                        if n - 1 in FF_AT:
                            feed_forward_residual(b - 1, FF_AT.index(n - 1))
                    if ahead:
                        row_max(b, n, 2)
                        row_max(b, n, 3)
                    if n in (21, 33, 45):
                        invert(b, n // UNIT - 1)
                    if n == 4 and not first:
                        invert(b - 1, 3)
                    if n % UNIT == 5 and (n < 36 or not last):
                        g = n // UNIT + 1
                        join_maxima(b + g // 4, g % 4)
                    for part in (1, 2):
                        if n - part in MT_AT and (n - part != MT_AT[3] or not last):
                            g = MT_AT.index(n - part) + 1
                            split_maxima(b + g // 4, g % 4, part)
                    if two_more:
                        if n in STATS_A_AT:
                            if n == STATS_A_AT[0]:
                                dve.wait_ge(x_loaded, 16 * b + 48)
                            norm_stats(0, xn, STATS_A_AT.index(n))
                        if n == 36:
                            norm_mean_var(b + 2, 0)
                            norm_add_eps(b + 2, 0)
                        for i in range(4):
                            if n == (37, 38, 38, 39)[i]:
                                normalise(b + 2, 0, xn, i)
                    if not first:
                        if n in (12, 13):
                            divide(b - 1, n - 12)
                        if n - 1 in WO_AT:
                            i = WO_AT.index(n - 1)
                            if any_yet(4 * b - 4 + i + 1):
                                dve.wait_ge(x1_done, 4 * b - 4 + i + 1)
                            norm_stats(1, xres, i)
                        if n == 19:
                            norm_mean_var(b - 1, 1)
                            norm_add_eps(b - 1, 1)
                        if 20 <= n < 24:
                            if not last:
                                dve.wait_ge(aT_ps, 4 * b + 8)
                            normalise(b - 1, 1, xres, n - 20)

            dve.wait_ge(cexp_done, 1)
            nc.vector.tensor_scalar(c_exp[:, :, :], c_exp[:, :, :], 1.0, None, ALU.add).then_inc(silu_step, 1)
            dve.wait_ge(silu_step, 1)
            nc.vector.reciprocal(c_exp[:, :, :], c_exp[:, :, :]).then_inc(silu_step, 1)
            dve.wait_ge(silu_step, 2)
            nc.vector.tensor_tensor(c_sb[:, :, :], c_sb[:, :, :], c_exp[:, :, :], ALU.mult).then_inc(silu_step, 1)
            dve.wait_ge(x_loaded, 16)
            for i in range(4):
                norm_stats(0, xn, i)
            dve.wait_ge(mod_ps, 8)
            for i in range(4):
                src = ps_misc[:, B * DH * i:B * DH * (i + 1)].rearrange("p (h b) -> p b h", h=DH)
                last = nc.vector.tensor_scalar(mod_cols[:, :, i, :], src, float(i % 2), None, ALU.add)
            last.then_inc(mod_ev, 1)
            dve.wait_ge(mod_ev, 1)
            norm_mean_var(0, 0)
            norm_add_eps(0, 0)
            for i in range(4):
                normalise(0, 0, xn, i)
            dve.wait_ge(mod_ps, 10)
            g_ps = ps_out[0:B, :]
            nc.vector.tensor_scalar(g_pos, g_ps, 0.25, None, ALU.max).then_inc(gate_step, 1)
            nc.vector.tensor_scalar(g_neg, g_ps, -0.25, None, ALU.min).then_inc(gate_step, 1)
            dve.wait_ge(gate_step, 2)
            nc.vector.scalar_tensor_tensor(out=g_pos, in0=g_ps, scalar=0.0, in1=g_pos,
                                           op0=ALU.is_ge, op1=ALU.mult).then_inc(gate_step, 1)
            nc.vector.scalar_tensor_tensor(out=g_neg, in0=g_ps, scalar=0.0, in1=g_neg,
                                           op0=ALU.is_lt, op1=ALU.mult).then_inc(gate_step, 1)
            dve.wait_ge(gate_step, 4)
            nc.vector.tensor_tensor(g_pos, g_pos, g_neg, ALU.add).then_inc(gate_step, 1)
            dve.wait_ge(b_loaded, 32)
            dve.wait_ge(consts_ready, 2)

            def bias_product(g):
                dve.wait_ge(w12_ps, 3 * g + 3)
                if any_yet(64 * (g // 2)):
                    dve.wait_ge(w12_stored[g % 2], 64 * (g // 2))
                nc.vector.tensor_tensor(bias_row[:, g % 2, :], ps_exp[0:1, (3 * g + 2) % 4, 0:D], b2_sb[:, g, :],
                                        ALU.add).then_inc(bias_ev, 1)

            bias_product(0)
            bias_product(1)
            for n in range(AHEAD):
                for h in range(4):
                    row_max(0, n - AHEAD, h)
                if n % 3 == 2:
                    bias_product(2 + n // 3)
                if n == UNIT - 1:
                    join_maxima(0, 0)
                if n == UNIT + 2:
                    for part in range(3):
                        split_maxima(0, 0, part)
                if n == 4:
                    dve.wait_ge(x_loaded, 32)
                if 4 <= n < 8:
                    norm_stats(0, xn, n - 4)
                if n == 8:
                    norm_mean_var(1, 0)
                    norm_add_eps(1, 0)
                if 9 <= n < 13:
                    normalise(1, 0, xn, n - 9)
            row(0, True, False, True)
            with dve.Fori(1, B - 2) as b:
                row(b, False, False, True)
            row(B - 2, False, False, False)
            row(B - 1, False, True, False)
            invert(B - 1, 3)
            divide(B - 1, 0)
            divide(B - 1, 1)
            for i in range(4):
                attention_residual(B - 1, i)
                if any_yet(4 * (B - 1) + i + 1):
                    dve.wait_ge(x1_done, 4 * (B - 1) + i + 1)
                norm_stats(1, xres, i)
            norm_mean_var(B - 1, 1)
            norm_add_eps(B - 1, 1)
            for i in range(4):
                normalise(B - 1, 1, xres, i)
            for i in range(4):
                feed_forward_residual(B - 1, i)

        @block.gpsimd
        def _(pool):
            def mask(b, n):
                pool.wait_ge(exp_done, 96 * b + 2 * n + 2)
                stand_alone(pool)
                v = probs[:, n % RING, :, 0:P]
                nc.gpsimd.affine_select(out=v, in_=v, compare_op=ALU.is_ge, fill=0.0, base=0,
                                        pattern=[[0, 4], [1, P]], channel_multiplier=-1).then_inc(masked, 1)

            def copy_values(b, g):
                u = 4 * b + g
                pool.wait_ge(v_ev, 4 * b + 4)
                if any_yet(12 * (u - 1)):
                    pool.wait_ge(pv_done, 12 * (u - 1))
                stand_alone(pool)
                nc.gpsimd.tensor_copy(v_ones[:, g % 2, :, :, 0:16],
                                      v_row[:, :, 64 * g:64 * g + 64].rearrange("p t (h d) -> p t h d", h=4)
                                      ).then_inc(v_copied, 1)

            def inverse_root(b, s):
                pool.wait_ge(c_step if s else a_step, 3 * b + 3)
                nc.gpsimd.tensor_tensor(rstd[:, s, :], rstd[:, s, :], exponent[:, :],
                                        ALU.pow).then_inc(c_rstd if s else a_rstd, 1)

            def rest_of_high(b, i):
                pool.wait_ge(qk_hi, 8 * b + i + 1)
                nc.gpsimd.tensor_tensor(rest[:, i % 2, :], rest[:, i % 2, :], parts[:, i % 4, 0, :],
                                        ALU.subtract).then_inc(qk_rest, 1)

            def low_part(b, i):
                pool.wait_ge(qk_mid, 8 * b + i + 1)
                nc.gpsimd.tensor_tensor(parts[:, i % 4, 2, :], rest[:, i % 2, :], parts[:, i % 4, 1, :],
                                        ALU.subtract).then_inc(qk_low, 1)

            def gate_weights(b, i):
                w, dh = i // 2, i % 2
                pool.wait_ge(c_loaded, 48 * b + 48)
                if any_yet(4 * b):
                    pool.wait_ge(wo_ps, 4 * b)
                src, dst = ((wo_sb, wo_gated), (ff_gated, ff_gated))[w]
                nc.gpsimd.tensor_tensor(dst[:, dh, :], src[:, dh, :], gates[:, D * w:D * w + D],
                                        ALU.mult).then_inc(gated, 1)

            def gate_bias(b):
                pool.wait_ge(gated, 4 * b + 4)
                nc.gpsimd.tensor_tensor(gates[:, 2 * D:3 * D], gates[:, 2 * D:3 * D], gates[:, D:2 * D],
                                        ALU.mult).then_inc(bias_gated, 1)

            def add_bias(b, i):
                pool.wait_ge(bias_gated, b + 1)
                pool.wait_ge(c_normed, 4 * b + i + 1)
                for t in (2 * i, 2 * i + 1):
                    nc.gpsimd.tensor_tensor(xres[:, t, :], xres[:, t, :], gates[:, 2 * D:3 * D],
                                            ALU.add).then_inc(biased, 1)

            def row(b, first, last, two_more):
                for n in range(STEPS):
                    if exp_step(n % UNIT)[3]:
                        mask(b, n)
                    if n == 36 and two_more:
                        inverse_root(b + 2, 0)
                    if not first:
                        if 8 <= n < 12:
                            gate_weights(b - 1, n - 8)
                        if n == 17:
                            gate_bias(b - 1)
                        if n == 19:
                            inverse_root(b - 1, 1)
                        if 23 <= n < 27:
                            add_bias(b - 1, n - 23)
                    if n % UNIT == 6 and (n < 36 or not last):
                        g = n // UNIT + 1
                        copy_values(b + g // 4, g % 4)
                    if not last:
                        if n - 1 in QK_AT:
                            rest_of_high(b + 1, QK_AT.index(n - 1))
                        if n - 2 in QK_AT:
                            low_part(b + 1, QK_AT.index(n - 2))

            bias_gated = sem("bias_gated")
            nc.gpsimd.memset(exponent[:, :], -0.5).then_inc(const_step, 1)
            nc.gpsimd.memset(ident[:, :], 0.0).then_inc(const_step, 1)
            nc.gpsimd.memset(causal[:, :], 0.0).then_inc(const_step, 1)
            pool.wait_ge(const_step, 3)
            nc.gpsimd.affine_select(out=ident[:, :], in_=ident[:, :], compare_op=ALU.not_equal, fill=1.0, base=0,
                                    pattern=[[-1, P]], channel_multiplier=1).then_inc(consts_ready, 1)
            nc.gpsimd.affine_select(out=causal[:, 384:512], in_=causal[:, 384:512], compare_op=ALU.is_ge,
                                    fill=-1.0e30, base=0, pattern=[[-1, P]],
                                    channel_multiplier=1).then_inc(consts_ready, 1)
            pool.wait_ge(consts_ready, 2)
            nc.gpsimd.memset(k_stack[96:99, :, :, :], 1.0).then_inc(ones_ready, 1)
            pool.wait_ge(ones_ready, 1)
            for s in range(2):
                nc.gpsimd.memset(v_ones[:, s, :, :, 16:32], 1.0).then_inc(ones_ready, 1)

            def load_w12(g):
                if any_yet(3 * (g - 1)):
                    pool.wait_ge(w12_ps, 3 * (g - 1))
                for m, w in enumerate((w1, w2)):
                    pool.dma_start(w12[:, g % 2, m], w[g].rearrange("(k p) n -> p k n", p=P)
                                   ).then_inc(w12_loaded[g % 2], 16)

            def store_product(g):
                pool.wait_ge(w12_ev, 2 * g + 2)
                pool.wait_ge(bias_ev, g + 1)
                for b in (2 * g, 2 * g + 1):
                    pool.dma_start(ff_dram[b], ff_out[:, g % 2]).then_inc(w12_stored[g % 2], 16)
                    pool.dma_start(gate_dram[b:b + 1, 2 * D:3 * D], bias_row[:, g % 2, :]).then_inc(w12_stored[g % 2], 16)

            load_w12(0)
            load_w12(1)
            inverse_root(0, 0)
            for i in range(8):
                rest_of_high(0, i)
                low_part(0, i)
            copy_values(0, 0)
            for g in range(G):
                store_product(g)
                if g + 2 < G:
                    load_w12(g + 2)
                if g == 2:
                    inverse_root(1, 0)
            row(0, True, False, True)
            with pool.Fori(1, B - 2) as b:
                row(b, False, False, True)
            row(B - 2, False, False, False)
            row(B - 1, False, True, False)
            for i in range(4):
                gate_weights(B - 1, i)
            gate_bias(B - 1)
            inverse_root(B - 1, 1)
            for i in range(4):
                add_bias(B - 1, i)


def kernel(L0_attn_x, L0_attn_WQ, L0_attn_WK, L0_attn_WV, L0_attn_WO, L0_ffn_W1, L0_ffn_b1, L0_ffn_W2, L0_ffn_b2,
           L0_c, L0_wmod):
    import numpy as np
    import concourse.bacc as bacc
    from concourse.bass_utils import run_bass_kernel_spmd

    b1 = np.asarray(L0_ffn_b1)
    groups, inner = b1.shape
    laid_out = {
        "x": np.asarray(L0_attn_x),
        "wq": np.asarray(L0_attn_WQ).T,
        "wk": np.asarray(L0_attn_WK).T,
        "wv": np.asarray(L0_attn_WV).T,
        "wo": np.asarray(L0_attn_WO).T,
        "w1": np.asarray(L0_ffn_W1),
        "b1": b1.reshape(groups, inner // P, P).transpose(2, 0, 1),
        "w2": np.asarray(L0_ffn_W2).transpose(0, 2, 1),
        "b2": np.asarray(L0_ffn_b2),
        "c": np.asarray(L0_c).T,
        "wmod": np.asarray(L0_wmod),
    }
    nc = bacc.Bacc("TRN2", target_bir_lowering=False, num_devices=1)
    arrays, args = {}, []
    for name, a in laid_out.items():
        a = np.ascontiguousarray(a)
        arrays[f"in_{name}"] = a
        args.append(nc.dram_tensor(f"in_{name}", a.shape, mybir.dt.from_np(a.dtype), kind="ExternalInput").ap())
    out = nc.dram_tensor("out_dram", laid_out["x"].shape, F32, kind="ExternalOutput").ap()
    adaln_block(nc, *args, out)
    result = run_bass_kernel_spmd(nc, [arrays], core_ids=[0])
    return result.results[0]["out_dram"]
```

```python
from contextlib import ExitStack

import concourse.bass as bass
from concourse import mybir

F32 = mybir.dt.float32
BF16 = mybir.dt.bfloat16
ALU = mybir.AluOpType
ACT = mybir.ActivationFunctionType
AX_X = mybir.AxisListType.X

P = 128
STEPS = 48
UNIT = 12
AHEAD = 18
LAG = 2
RING = 4

QK_AT = [1, 3, 5, 8, 10, 13, 20, 22]
QK_REST_AT = [3, 5, 7, 10, 12, 15, 22, 24]
QK_MID_AT = [3, 5, 7, 10, 13, 15, 22, 25]
WO_AT = [14, 15, 16, 17]
CT_AT = [23, 24, 25, 26]
FF_AT = [27, 28, 29, 31]
V_AT = [32, 34, 37, 38]
AT_AT = [43, 44, 45, 46]
MT_AT = [6, 18, 30, 42]
STATS_A_AT = [31, 32, 33, 35]


def exp_step(k):
    c, j = (0, k) if k < 4 else (1, k - 4)
    diagonal = j >= 4 * c
    width = 512 - 128 * (j - 4 * c) if diagonal else 512
    return c, j, width, diagonal


def max_step(k):
    if k < 4:
        return k, 0, 128 * (k + 1), True
    t, half = 4 + (k - 4) // 2, (k - 4) % 2
    return t, half, (128 * (t - 3) if half else 512), half == 1


def masks_before(k):
    return sum(exp_step(i)[3] for i in range(k + 1))


def adaln_block(nc, x, wq, wk, wv, wo, w1, b1, w2, b2, cT, wmod, out):
    B, S, D = x.shape
    G, O = w1.shape[0], w1.shape[1]
    NT = S // P
    DH = D // P
    KT = O // P
    EPS = 1e-5
    assert (S, D, NT, DH, KT) == (1024, 256, 8, 2, 8) and B == 2 * G

    qk_dram = nc.dram_tensor("qk_parts", [B, 2, 3, D, S], BF16, kind="Internal").ap()
    nmax_dram = nc.dram_tensor("nmax_parts", [B, 4, 3, 32, P], BF16, kind="Internal").ap()
    den_dram = nc.dram_tensor("denominators", [B, 4, 4, S], F32, kind="Internal").ap()
    rden_dram = nc.dram_tensor("reciprocals", [B, 4, 4, S], F32, kind="Internal").ap()
    gate_dram = nc.dram_tensor("gates", [B, 3 * D], F32, kind="Internal").ap()
    ff_dram = nc.dram_tensor("ff_product", [B, P, DH, D], F32, kind="Internal").ap()

    with ExitStack() as ctx:
        def sb(name, shape, dt=F32):
            return ctx.enter_context(nc.sbuf_tensor(name, shape, dt))

        def ps(name, shape):
            return ctx.enter_context(nc.psum_tensor(name, shape, F32))

        def sem(name):
            return ctx.enter_context(nc.semaphore(name))

        q_stack = sb("q_stack", [P, RING, 4, S], BF16)
        k_stack = sb("k_stack", [P, RING, 4, S], BF16)
        probs = sb("probs", [P, RING, 4, 512])
        xn = sb("xn", [P, NT, D])
        xres = sb("xres", [P, NT, D])
        hT_a = sb("hT_a", [P, DH, S])
        hT_c = sb("hT_c", [P, DH, S])
        v_row = sb("v_row", [P, NT, D])
        v_ones = sb("v_ones", [P, 2, NT, 4, 32])
        o_both = sb("o_both", [P, 2, DH, S])
        o_num, o_rden = o_both[:, 0], o_both[:, 1]
        den_cols = sb("den_cols", [P, 2, 32])
        o_raw = sb("o_raw", [P, 2, S])
        parts = sb("parts", [P, 4, 3, 512], BF16)
        rest = sb("rest", [P, 2, 512])
        wq_sb, wk_sb, wv_sb, wo_sb = (sb(n, [P, DH, D]) for n in ("wq_sb", "wk_sb", "wv_sb", "wo_sb"))
        wo_gated = sb("wo_gated", [P, DH, D])
        ff_gated = sb("ff_gated", [P, DH, D])
        gates = sb("gates_sb", [P, 3 * D])
        causal = sb("causal", [P, 512])
        ident = sb("ident", [P, P])
        scratch = sb("scratch", [P, 3, 512], BF16)
        mod_cols = sb("mod_cols", [P, B, 4, DH])
        mod_a = sb("mod_a", [P, 4, DH])
        mod_c = sb("mod_c", [P, 4, DH])
        exponent = sb("exponent", [P, NT])
        stats = sb("stats", [P, 2, NT, 6])
        mean_var = sb("mean_var", [P, 2, NT, 2])
        rstd = sb("rstd", [P, 2, NT])
        mx = sb("mx", [P, 2, 4, NT])
        mx_low = sb("mx_low", [P, 2, 4, 4])
        nmax = sb("nmax", [32, 3, P], BF16)
        nrest = sb("nrest", [32, P])
        c_sb = sb("c_sb", [P, DH, B])
        c_exp = sb("c_exp", [P, DH, B])

        bias_halves = gates[:, 2 * D:3 * D].rearrange("q (p h) -> q h p", h=DH)

        wmod_sb = o_both[:, :, :, :].rearrange("p a h s -> p (a h s)")[:, 0:DH * 6 * D].rearrange(
            "p (h n) -> p h n", h=DH)
        w12 = probs[:, :, :, :].rearrange("p r h q -> p (r h q)").rearrange(
            "p (s m k n) -> p s m k n", s=2, m=2, k=KT)
        ff_out = hT_c[:, 0, :].rearrange("p (s h n) -> p s h n", s=2, h=DH)
        bias_cols = hT_c[:, 1, 0:2 * DH].rearrange("p (s h) -> p s h", s=2)
        b1_sb = hT_c[:, 1, 2 * D:2 * D + G * KT].rearrange("p (g k) -> p g k", g=G)
        bias_sums = xres[:, 1:3, :]
        g_pos, g_neg = o_raw[0:B, 0, 0:2 * D], o_raw[0:B, 1, 0:2 * D]
        b2_sb = xres[:, 0, 0:G * DH].rearrange("p (g h) -> p g h", g=G)

        ps_max = ps("ps_max", [P, 3, 512])
        ps_exp = ps("ps_exp", [P, 3, 512])
        ps_out = ps("ps_out", [P, 512])
        ps_misc = ps("ps_misc", [P, 512])

        def stage_c_bank(b, i):
            return ps_exp[:, i - 1, :] if isinstance(b, int) and b == B - 1 and i > 0 else ps_misc[:, :]

        mod_loaded, x0_weights_loaded, b_loaded = sem("mod_loaded"), sem("weights_loaded"), sem("b_loaded")
        x_loaded, c_loaded, w12_loaded = sem("x_loaded"), sem("c_loaded"), [sem("w12_loaded0"), sem("w12_loaded1")]
        consts_ready, const_step, ones_ready = sem("consts_ready"), sem("const_step"), sem("ones_ready")
        cexp_done, silu_step, mod_ps, mod_ev, gate_step, gate_stored = (
            sem(n) for n in ("cexp_done", "silu_step", "mod_ps", "mod_ev", "gate_step", "gate_stored"))
        w12_ps, w12_ev, bias_summed, bias_ev = (sem(n) for n in ("w12_ps", "w12_ev", "bias_summed", "bias_ev"))
        w12_stored = [sem("w12_stored0"), sem("w12_stored1")]
        a_rstd, c_rstd = sem("a_rstd"), sem("c_rstd")
        a_step, a_normed, aT_ps, aT_ev = (sem(n) for n in ("a_step", "a_normed", "aT_ps", "aT_ev"))
        qk_ps, qk_hi, qk_copied, qk_rest, qk_mid, qk_low = (
            sem(n) for n in ("qk_ps", "qk_hi", "qk_copied", "qk_rest", "qk_mid", "qk_low"))
        qk_stored = [sem(f"qk_stored{i}") for i in range(4)]
        stack_loaded = [sem(f"stack_loaded{i}") for i in range(RING)]
        v_ps, v_ev, v_copied = sem("v_ps"), sem("v_ev"), sem("v_copied")
        smax_ps, smax_done, mx_joined, mT_ps, nmax_step, nmax_stored, nmax_loaded = (
            sem(n) for n in ("smax_ps", "smax_done", "mx_joined", "mT_ps", "nmax_step", "nmax_stored", "nmax_loaded"))
        sexp_ps, exp_done, masked, pv_done, o_copied = (
            sem(n) for n in ("sexp_ps", "exp_done", "masked", "pv_done", "o_copied"))
        num_moved, rden_spread = ([sem(f"{n}{i}") for i in range(2)] for n in ("num_moved", "rden_spread"))
        den_stored, den_loaded, inverted, rden_stored = (
            sem(n) for n in ("den_stored", "den_loaded", "inverted", "rden_stored"))
        gated, divided, wo_ps, x1_done, c_step, c_normed, cT_ps, cT_ev, biased, ff_ps, ff_done, out_stored = (
            sem(n) for n in ("gated", "divided", "wo_ps", "x1_done", "c_step", "c_normed", "cT_ps", "cT_ev",
                             "biased", "ff_ps", "ff_done", "out_stored"))

        waits_met = sem("waits_met")

        def stand_alone(eng):
            eng.sem_inc(waits_met, 1)

        def any_yet(count):
            return not isinstance(count, int) or count > 0

        block = ctx.enter_context(nc.Block())

        @block.sync
        def _(sp):
            def load_stack(b, g):
                for s in range(4):
                    if any_yet(32 * b + (16 if g < 2 else 32)):
                        sp.wait_ge(qk_stored[s], 32 * b + (16 if g < 2 else 32))
                        stand_alone(sp)
                if any_yet(192 * b - 192 + 48 * (g + 1)):
                    sp.wait_ge(sexp_ps, 192 * b - 192 + 48 * (g + 1))
                    stand_alone(sp)
                for r, (qp, kp) in enumerate([(0, 0), (0, 1), (0, 2), (1, 0), (1, 1), (2, 0)]):
                    for stack, m, part in ((q_stack, 0, qp), (k_stack, 1, kp)):
                        sp.dma_start(
                            stack[16 * r:16 * r + 16, g, :, :],
                            qk_dram[b, m, part, 64 * g:64 * g + 64, :].rearrange("(h d) s -> d h s", d=16),
                        ).then_inc(stack_loaded[g], 16)

            def move_maxima(b, g):
                u = 4 * b + g
                sp.wait_ge(nmax_step, 4 * u + 4)
                stand_alone(sp)
                sp.dma_start(nmax_dram[b, g].rearrange("t r q -> r t q"), nmax[:, :, :]).then_inc(nmax_stored, 16)
                sp.wait_ge(nmax_stored, 16 * u + 16)
                stand_alone(sp)
                if any_yet(48 * u - 144):
                    sp.wait_ge(sexp_ps, 48 * u - 144)
                    stand_alone(sp)
                sp.dma_start(
                    q_stack[96:99, g, :, :].rearrange("p h s -> p (h s)"),
                    nmax_dram[b, g].rearrange("t r q -> t (r q)"),
                ).then_inc(nmax_loaded, 16)

            def store_parts(b, i):
                m, oh, half = (i // 2) % 2, i // 4, i % 2
                sp.wait_ge(qk_low, 8 * b + i + 1)
                stand_alone(sp)
                sp.dma_start(
                    qk_dram[b, m, :, P * oh:P * oh + P, 512 * half:512 * half + 512].rearrange("t p s -> p t s"),
                    parts[:, i % 4, :, :],
                ).then_inc(qk_stored[i % 4], 16)

            def move_output(b, g):
                u = 4 * b + g
                sp.wait_ge(o_copied, 2 * u + 2)
                stand_alone(sp)
                sp.dma_start(den_dram[b, g], o_raw[16:P:32, g % 2, :]).then_inc(den_stored, 16)
                if any_yet(4 * b):
                    sp.wait_ge(wo_ps, 4 * b)
                    stand_alone(sp)
                for h in range(4):
                    at = 64 * (g % 2) + 16 * h
                    sp.dma_start(o_num[at:at + 16, g // 2, :], o_raw[32 * h:32 * h + 16, g % 2, :]
                                 ).then_inc(num_moved[g % 2], 16)
                sp.wait_ge(den_stored, 16 * u + 16)
                stand_alone(sp)
                sp.dma_start(den_cols[:, g % 2, :], den_dram[b, g].rearrange("h (p c) -> (h p) c", c=32)
                             ).then_inc(den_loaded, 16)

            def spread_reciprocals(b, g):
                u = 4 * b + g
                sp.wait_ge(inverted, u + 1)
                stand_alone(sp)
                sp.dma_start(rden_dram[b, g].rearrange("h (p c) -> (h p) c", c=32), den_cols[:, g % 2, :]
                             ).then_inc(rden_stored, 16)
                if any_yet(2 * b):
                    sp.wait_ge(divided, 2 * b)
                    stand_alone(sp)
                sp.wait_ge(rden_stored, 16 * u + 16)
                stand_alone(sp)
                for h in range(4):
                    at = 64 * (g % 2) + 16 * h
                    sp.dma_start(o_rden[at:at + 16, g // 2, :], rden_dram[b, g, h].partition_broadcast(16)
                                 ).then_inc(rden_spread[g % 2], 16)

            def load_x(b):
                if any_yet(4 * b):
                    sp.wait_ge(aT_ps, 4 * b)
                    stand_alone(sp)
                if any_yet(4 * b - 8):
                    sp.wait_ge(cT_ps, 4 * b - 8)
                    stand_alone(sp)
                sp.dma_start(xn[:, :, :], x[b].rearrange("(t p) d -> p t d", p=P)).then_inc(x_loaded, 16)

            def load_c(b):
                if any_yet(4 * b):
                    sp.wait_ge(gated, 4 * b)
                    stand_alone(sp)
                if any_yet(8 * b):
                    sp.wait_ge(biased, 8 * b)
                    stand_alone(sp)
                sp.dma_start(gates[:, :], gate_dram[b].partition_broadcast(P)).then_inc(c_loaded, 16)
                if any_yet(4 * b):
                    sp.wait_ge(ff_ps, 4 * b)
                    stand_alone(sp)
                sp.dma_start(ff_gated[:, :, :], ff_dram[b]).then_inc(c_loaded, 16)
                if any_yet(16 * b):
                    sp.wait_ge(out_stored, 16 * b)
                    stand_alone(sp)
                sp.dma_start(xres[:, :, :], x[b].rearrange("(t p) d -> p t d", p=P)).then_inc(c_loaded, 16)

            def store_out(b):
                sp.wait_ge(ff_done, 4 * b + 4)
                stand_alone(sp)
                sp.dma_start(out[b].rearrange("(t p) d -> p t d", p=P), xres[:, :, :]).then_inc(out_stored, 16)

            def row(b, first, last, two_more):
                for n in range(STEPS):
                    if n == 28 and two_more:
                        load_x(b + 2)
                    if n == 0:
                        if not first:
                            load_c(b - 1)
                            load_stack(b, 3)
                    if n == 2 and not first:
                        move_output(b - 1, 3)
                    if n - 2 in MT_AT:
                        g = MT_AT.index(n - 2) + 1
                        if g < 4 or not last:
                            move_maxima(b + g // 4, g % 4)
                    if n in (19, 31, 43):
                        move_output(b, n // UNIT - 1)
                    if n in (21, 33, 45):
                        spread_reciprocals(b, n // UNIT - 1)
                    if n == 5 and not first:
                        spread_reciprocals(b - 1, 3)
                    if n - 2 in QK_MID_AT and not last:
                        store_parts(b + 1, QK_MID_AT.index(n - 2))
                    if n in (18, 27, 38) and not last:
                        load_stack(b + 1, (18, 27, 38).index(n))
                    if n == 33 and not first:
                        store_out(b - 1)

            sp.dma_start(c_sb[:, :, :], cT.rearrange("(h p) b -> p h b", p=P)).then_inc(mod_loaded, 16)
            load_x(0)
            sp.dma_start(wmod_sb, wmod.rearrange("(h p) n -> p h n", p=P)).then_inc(mod_loaded, 16)
            for buf, w in ((wq_sb, wq), (wk_sb, wk), (wv_sb, wv), (wo_sb, wo)):
                sp.dma_start(buf[:, :, :], w.rearrange("(h p) n -> p h n", p=P)).then_inc(x0_weights_loaded, 16)
            sp.dma_start(b1_sb[:, :, :], b1).then_inc(b_loaded, 16)
            sp.dma_start(b2_sb, b2).then_inc(b_loaded, 16)
            sp.wait_ge(gate_step, 5)
            stand_alone(sp)
            sp.dma_start(gate_dram[:, 0:2 * D], g_pos).then_inc(gate_stored, 16)
            for i in range(4):
                store_parts(0, i)
            load_stack(0, 0)
            load_stack(0, 1)
            for i in range(4, 8):
                store_parts(0, i)
            load_x(1)
            move_maxima(0, 0)
            load_stack(0, 2)
            load_stack(0, 3)
            sp.wait_ge(mod_ps, 10)
            stand_alone(sp)
            sp.wait_ge(gate_stored, 16)
            stand_alone(sp)
            for s in range(2):
                sp.wait_ge(w12_stored[s], 64 * (G // 2))
                stand_alone(sp)
            row(0, True, False, True)
            with sp.Fori(1, B - 2) as b:
                row(b, False, False, True)
            row(B - 2, False, False, False)
            row(B - 1, False, True, False)
            load_c(B - 1)
            move_output(B - 1, 3)
            spread_reciprocals(B - 1, 3)
            store_out(B - 1)
            sp.wait_ge(out_stored, 16 * B)
            stand_alone(sp)
            for s in range(4):
                sp.wait_ge(qk_stored[s], 32 * B)
                stand_alone(sp)
            for s in (nmax_stored, den_stored, rden_stored):
                sp.wait_ge(s, 64 * B)
                stand_alone(sp)

        @block.tensor
        def _(pe):
            copied, count = mod_ev, 1

            def misc_copied_by(s, value):
                nonlocal copied, count
                copied, count = s, value

            def scores_for_max(b, n, h):
                g, k = divmod(n + AHEAD, UNIT)
                t, half, width, _ = max_step(k)
                if k == 0 and h == 0:
                    pe.wait_ge(stack_loaded[g % 4], 192 * (b + g // 4) + 192)
                at = 4 * (STEPS * b + n + AHEAD) + h
                if any_yet(at - 2):
                    pe.wait_ge(smax_done, at - 2)
                nc.tensor.matmul(ps_max[:, (4 * (n + AHEAD) + h) % 3, 0:width], q_stack[0:96, g % 4, h, P * t:P * t + P],
                                 k_stack[0:96, g % 4, h, 512 * half:512 * half + width],
                                 start=True, stop=True).then_inc(smax_ps, 1)

            def scores_for_exp(b, n, pair):
                g, k = divmod(n, UNIT)
                c, j, width, _ = exp_step(k)
                if k == 0 and pair == 0:
                    pe.wait_ge(nmax_loaded, 64 * b + 16 * g + 16)
                for h in (2 * pair, 2 * pair + 1):
                    q0 = 512 * c + 512 - width
                    if any_yet(192 * b + 4 * n + h - 2):
                        pe.wait_ge(exp_done, 192 * b + 4 * n + h - 2)
                    nc.tensor.matmul(ps_exp[:, (4 * n + h) % 3, 0:width], k_stack[0:99, g, h, P * j:P * j + P],
                                     q_stack[0:99, g, h, q0:q0 + width],
                                     start=True, stop=True).then_inc(sexp_ps, 1)

            def values(b, n):
                g, k = divmod(n, UNIT)
                c, j, width, diagonal = exp_step(k)
                pe.wait_ge(exp_done, 192 * b + 4 * n + 4)
                if diagonal:
                    if any_yet(32 * b + 8 * g + masks_before(k)):
                        pe.wait_ge(masked, 32 * b + 8 * g + masks_before(k))
                if k == 0:
                    pe.wait_ge(v_copied, 4 * b + g + 1)
                if j == 0:
                    if any_yet(8 * b + 2 * g + c):
                        pe.wait_ge(o_copied, 8 * b + 2 * g + c)
                for h in range(4):
                    last = nc.tensor.matmul(ps_out[32 * h:32 * h + 32, 512 - width:512],
                                            v_ones[:, g % 2, j, h, :], probs[:, n % RING, h, 0:width],
                                            start=(j == 0), stop=(k in (3, 11)))
                last.then_inc(pv_done, 1)

            def transpose_normed(b, i, normed, ps_sem, ev_sem, bank=ps_misc):
                half, dh = divmod(i, 2)
                pe.wait_ge(normed, 4 * b + 2 * half + 2)
                if bank is ps_misc:
                    pe.wait_ge(copied, count)
                    misc_copied_by(ev_sem, 4 * b + i + 1)
                for t in range(4):
                    last = nc.tensor.transpose(bank[:, P * t:P * t + P],
                                               xn[:, 4 * half + t, P * dh:P * dh + P], ident[:, :])
                last.then_inc(ps_sem, 1)

            def project_qk(b, i):
                m, oh, half = (i // 2) % 2, i // 4, i % 2
                pe.wait_ge(aT_ev, 4 * b + 2 * half + 2)
                pe.wait_ge(copied, count)
                misc_copied_by(qk_copied, 8 * b + i + 1)
                w = wk_sb if m else wq_sb
                for dh in range(DH):
                    last = nc.tensor.matmul(ps_misc[:, :], w[:, dh, P * oh:P * oh + P],
                                            hT_a[:, dh, 512 * half:512 * half + 512],
                                            start=(dh == 0), stop=(dh == DH - 1))
                last.then_inc(qk_ps, 1)

            def by_token(i, hT, w, rows, bank=ps_misc):
                for t in range(2):
                    for dh in range(DH):
                        last = nc.tensor.matmul(bank[:, D * t:D * t + D],
                                                hT[:, dh, P * (2 * i + t):P * (2 * i + t) + P], w[:, dh, :],
                                                start=(dh == 0), stop=(dh == DH - 1))
                last.then_inc(rows, 1)

            def project_v(b, i):
                pe.wait_ge(aT_ev, 4 * b + 4)
                pe.wait_ge(copied, count)
                misc_copied_by(v_ev, 4 * b + i + 1)
                by_token(i, hT_a, wv_sb, v_ps)

            def project_out(b, i, bank=ps_misc):
                pe.wait_ge(divided, 2 * b + 2)
                pe.wait_ge(gated, 4 * b + 2)
                if bank is ps_misc:
                    pe.wait_ge(copied, count)
                    misc_copied_by(x1_done, 4 * b + i + 1)
                by_token(i, o_num, wo_gated, wo_ps, bank)

            def feed_forward(b, i, bank=ps_misc):
                pe.wait_ge(cT_ev, 4 * b + (2 if i < 2 else 4))
                pe.wait_ge(gated, 4 * b + 4)
                if bank is ps_misc:
                    pe.wait_ge(copied, count)
                    misc_copied_by(ff_done, 4 * b + i + 1)
                by_token(i, hT_c, ff_gated, ff_ps, bank)

            def maxima_to_rows(b, g):
                u = 4 * b + g
                pe.wait_ge(mx_joined, u + 1)
                pe.wait_ge(copied, count)
                misc_copied_by(nmax_step, 4 * u + 2)
                nc.tensor.matmul(ps_misc[0:32, 0:P], mx[:, g % 2, :, :].rearrange("p h t -> p (h t)"), ident[:, :],
                                 start=True, stop=True).then_inc(mT_ps, 1)

            def ff_product(i):
                g, what = divmod(i, 3)
                if any_yet(32 * (g // 2 + 1)):
                    pe.wait_ge(w12_loaded[g % 2], 32 * (g // 2 + 1))
                if what < 2:
                    if any_yet(2 * g - 1 + what):
                        pe.wait_ge(w12_ev, 2 * g - 1 + what)
                elif any_yet(g):
                    pe.wait_ge(bias_ev, g)
                w1t, w2t = w12[:, g % 2, 0], w12[:, g % 2, 1]
                for kt in range(KT if what < 2 else 0):
                    last = nc.tensor.matmul(ps_exp[:, what, 0:D], w1t[:, kt, P * what:P * what + P], w2t[:, kt, :],
                                            start=(kt == 0), stop=(kt == KT - 1))
                if what == 2:
                    pe.wait_ge(bias_summed, KT * g + KT)
                for dh in range(DH if what == 2 else 0):
                    last = nc.tensor.matmul(ps_exp[:, 2, dh:dh + 1], bias_sums[:, g % 2, P * dh:P * dh + P],
                                            v_ones[:, 0, 0, 0, 16:17], start=True, stop=True)
                last.then_inc(w12_ps, 1)

            def ff_half(g, half):
                ff_product(3 * g + half)
                if half == 1:
                    ff_product(3 * g + 2)

            def row(b, first, last, two_more):
                if last:
                    misc_copied_by(nmax_step, 16 * b + 2)
                else:
                    misc_copied_by(aT_ev, 4 * b + 8)
                for n in range(STEPS):
                    ahead = (n + AHEAD) // UNIT < 4 or not last
                    if ahead:
                        scores_for_max(b, n, 0)
                    scores_for_exp(b, n, 0)
                    if ahead:
                        scores_for_max(b, n, 1)
                    if n >= LAG:
                        values(b, n - LAG)
                    elif not first:
                        values(b - 1, n - LAG + STEPS)
                    if ahead:
                        scores_for_max(b, n, 2)
                    scores_for_exp(b, n, 1)
                    if ahead:
                        scores_for_max(b, n, 3)
                    if n in MT_AT:
                        g = MT_AT.index(n) + 1
                        if g < 4 or not last:
                            maxima_to_rows(b + g // 4, g % 4)
                    if not first:
                        if n in WO_AT:
                            project_out(b - 1, WO_AT.index(n))
                        if n in CT_AT:
                            transpose_normed(b - 1, CT_AT.index(n), c_normed, cT_ps, cT_ev)
                        if n in FF_AT:
                            feed_forward(b - 1, FF_AT.index(n))
                    if two_more and n in AT_AT:
                        transpose_normed(b + 2, AT_AT.index(n), a_normed, aT_ps, aT_ev)
                    if not last:
                        if n in QK_AT:
                            project_qk(b + 1, QK_AT.index(n))
                        if n in V_AT:
                            project_v(b + 1, V_AT.index(n))

            pe.wait_ge(mod_loaded, 32)
            pe.wait_ge(silu_step, 3)
            for i, which in enumerate((0, 1, 3, 4)):
                for oh in range(DH):
                    at = B * (DH * i + oh)
                    for dh in range(DH):
                        last = nc.tensor.matmul(ps_misc[:, at:at + B],
                                                wmod_sb[:, dh, D * which + P * oh:D * which + P * oh + P],
                                                c_sb[:, dh, :], start=(dh == 0), stop=(dh == DH - 1))
                    last.then_inc(mod_ps, 1)
            for i, which in enumerate((2, 5)):
                for dh in range(DH):
                    last = nc.tensor.matmul(ps_out[0:B, D * i:D * i + D], c_sb[:, dh, :],
                                            wmod_sb[:, dh, D * which:D * which + D],
                                            start=(dh == 0), stop=(dh == DH - 1))
                last.then_inc(mod_ps, 1)
            pe.wait_ge(consts_ready, 2)
            for i in range(4):
                transpose_normed(0, i, a_normed, aT_ps, aT_ev)
            pe.wait_ge(x0_weights_loaded, 64)
            pe.wait_ge(ones_ready, 3)
            for i in range(8):
                project_qk(0, i)
                if i % 4 == 3:
                    ff_half(0, i // 4)
            ff_half(1, 0)
            for n in range(AHEAD):
                for h in range(4):
                    scores_for_max(0, n - AHEAD, h)
                if n + 3 < 2 * G:
                    ff_half((n + 3) // 2, (n + 3) % 2)
                if 9 <= n < 13:
                    project_v(0, n - 9)
                if n == UNIT + 1:
                    maxima_to_rows(0, 0)
                if n > UNIT + 1:
                    transpose_normed(1, n - UNIT - 2, a_normed, aT_ps, aT_ev)
            pe.wait_ge(w12_ev, 2 * G)
            pe.wait_ge(bias_ev, G)
            pe.wait_ge(gate_step, 5)
            row(0, True, False, True)
            with pe.Fori(1, B - 2) as b:
                row(b, False, False, True)
            row(B - 2, False, False, False)
            row(B - 1, False, True, False)
            for n in range(STEPS - LAG, STEPS):
                values(B - 1, n)
            banks = [ps_misc] + [ps_exp[:, i, :] for i in range(3)]
            for i in range(4):
                project_out(B - 1, i, banks[i])
            for i in range(4):
                transpose_normed(B - 1, i, c_normed, cT_ps, cT_ev, banks[i])
            for i in range(4):
                feed_forward(B - 1, i, banks[i])

        @block.scalar
        def _(act):
            def exp(b, n, pair):
                width = exp_step(n % UNIT)[2]
                if pair == 0 and any_yet(48 * b + n - RING + 1):
                    act.wait_ge(pv_done, 48 * b + n - RING + 1)
                for h in (2 * pair, 2 * pair + 1):
                    act.wait_ge(sexp_ps, 192 * b + 4 * n + h + 1)
                    nc.scalar.activation(probs[:, n % RING, h, 0:width], ps_exp[:, (4 * n + h) % 3, 0:width],
                                         ACT.Exp, scale=0.25).then_inc(exp_done, 1)

            def copy_output(b, n):
                g, k = divmod(n, UNIT)
                c = exp_step(k)[0]
                act.wait_ge(pv_done, 48 * b + n + 1)
                if any_yet(128 * b + 64 * (g // 2)):
                    act.wait_ge(num_moved[g % 2], 128 * b + 64 * (g // 2))
                if any_yet(16 * (4 * b + g - 1)):
                    act.wait_ge(den_stored, 16 * (4 * b + g - 1))
                nc.scalar.copy(o_raw[:, g % 2, 512 * c:512 * c + 512], ps_out[:, :]).then_inc(o_copied, 1)

            def modulate(b, i, ps_sem, ev_sem, mod, hT, mod_ready, free, free_at, bank):
                half, dh = divmod(i, 2)
                act.wait_ge(ps_sem, 4 * b + i + 1)
                act.wait_ge(mod_ready, 3 * b + 2)
                for s, value in zip(free, free_at):
                    if any_yet(value):
                        act.wait_ge(s, value)
                nc.scalar.activation(hT[:, dh, 512 * half:512 * half + 512], bank, ACT.Identity,
                                     scale=mod[:, 1, dh:dh + 1], bias=mod[:, 0, dh:dh + 1]).then_inc(ev_sem, 1)

            def modulate_a(b, i):
                modulate(b, i, aT_ps, aT_ev, mod_a, hT_a, a_step, (v_ps,), (4 * b,), ps_misc[:, :])

            def modulate_c(b, i):
                modulate(b, i, cT_ps, cT_ev, mod_c[:, 2:4, :], hT_c, c_step, (ff_ps,), (4 * b,), stage_c_bank(b, i))

            def copy_qk(b, i):
                act.wait_ge(qk_ps, 8 * b + i + 1)
                if any_yet(8 * b + i - 1):
                    act.wait_ge(qk_low, 8 * b + i - 1)
                nc.scalar.copy(rest[:, i % 2, :], ps_misc[:, :]).then_inc(qk_copied, 1)

            def high_part(b, i):
                act.wait_ge(qk_copied, 8 * b + i + 1)
                if any_yet(32 * b + 16 * (i // 4)):
                    act.wait_ge(qk_stored[i % 4], 32 * b + 16 * (i // 4))
                nc.scalar.copy(parts[:, i % 4, 0, :], rest[:, i % 2, :]).then_inc(qk_hi, 1)

            def middle_part(b, i):
                act.wait_ge(qk_rest, 8 * b + i + 1)
                nc.scalar.copy(parts[:, i % 4, 1, :], rest[:, i % 2, :]).then_inc(qk_mid, 1)

            def copy_v(b, i):
                act.wait_ge(v_ps, 4 * b + i + 1)
                if any_yet(4 * b):
                    act.wait_ge(v_copied, 4 * b)
                nc.scalar.copy(v_row[:, 2 * i:2 * i + 2, :],
                               ps_misc[:, :].rearrange("p (t d) -> p t d", t=2)).then_inc(v_ev, 1)

            def row(b, first, last, two_more):
                for n in range(STEPS):
                    if two_more and n - 1 in AT_AT:
                        modulate_a(b + 2, AT_AT.index(n - 1))
                    if not last and n - 1 in QK_AT:
                        copy_qk(b + 1, QK_AT.index(n - 1))
                    if not last and n - 1 in V_AT:
                        copy_v(b + 1, V_AT.index(n - 1))
                    if not first and n - 1 in CT_AT:
                        modulate_c(b - 1, CT_AT.index(n - 1))
                    exp(b, n, 0)
                    if (n - LAG) % UNIT in (3, 11):
                        if n >= LAG:
                            copy_output(b, n - LAG)
                        elif not first:
                            copy_output(b - 1, n - LAG + STEPS)
                    exp(b, n, 1)
                    if not last:
                        if n - 1 in QK_AT:
                            high_part(b + 1, QK_AT.index(n - 1))
                        if n in QK_MID_AT:
                            middle_part(b + 1, QK_MID_AT.index(n))

            def product_copy(g, what):
                act.wait_ge(w12_ps, 3 * g + what + 1)
                if any_yet(64 * (g // 2)):
                    act.wait_ge(w12_stored[g % 2], 64 * (g // 2))
                nc.scalar.copy(ff_out[:, g % 2, what, :], ps_exp[:, what, 0:D]).then_inc(w12_ev, 1)

            act.wait_ge(mod_loaded, 32)
            nc.scalar.activation(c_exp[:, :, :], c_sb[:, :, :], ACT.Exp, scale=-1.0).then_inc(cexp_done, 1)
            for i in range(4):
                modulate_a(0, i)
            for i in range(8):
                copy_qk(0, i)
                high_part(0, i)
                if i > 0:
                    middle_part(0, i - 1)
                if i % 4 == 3:
                    product_copy(0, i // 4)
            middle_part(0, 7)
            product_copy(1, 0)
            for n in range(AHEAD):
                if n + 3 < 2 * G:
                    product_copy((n + 3) // 2, (n + 3) % 2)
                if 9 <= n < 13:
                    copy_v(0, n - 9)
                if n > UNIT + 1:
                    modulate_a(1, n - UNIT - 2)
            act.wait_ge(w12_ps, 3 * G)
            for s in range(2):
                act.wait_ge(w12_stored[s], 64 * (G // 2))
            row(0, True, False, True)
            with act.Fori(1, B - 2) as b:
                row(b, False, False, True)
            row(B - 2, False, False, False)
            row(B - 1, False, True, False)
            copy_output(B - 1, STEPS - 1)
            for i in range(4):
                modulate_c(B - 1, i)

        @block.vector
        def _(dve):
            def row_max(b, n, h):
                g, k = divmod(n + AHEAD, UNIT)
                t, half, width, diagonal = max_step(k)
                bank = (4 * (n + AHEAD) + h) % 3
                if k == 0 and h == 0:
                    if any_yet(4 * b + g - 1):
                        dve.wait_ge(mT_ps, 4 * b + g - 1)
                dve.wait_ge(smax_ps, 4 * STEPS * b + 4 * (n + AHEAD) + h + 1)
                if diagonal:
                    stand_alone(dve)
                    ins = nc.vector.tensor_tensor_reduce(
                        scratch[:, bank, 0:width], ps_max[:, bank, 0:width], causal[:, 512 - width:512],
                        1.0, -3.0e38, ALU.add, ALU.max, mx[:, g % 2, h, t:t + 1])
                else:
                    ins = nc.vector.tensor_reduce(mx_low[:, g % 2, h, t - 4:t - 3], ps_max[:, bank, :],
                                                  AX_X, ALU.max)
                ins.then_inc(smax_done, 1)

            def join_maxima(b, g):
                u = 4 * b + g
                dve.wait_ge(smax_done, 48 * u + 48)
                nc.vector.tensor_tensor(mx[:, g % 2, :, 4:8], mx[:, g % 2, :, 4:8], mx_low[:, g % 2, :, :],
                                        ALU.max).then_inc(mx_joined, 1)

            def split_maxima(b, g, part):
                u = 4 * b + g
                m = ps_misc[0:32, 0:P]
                if part == 0:
                    dve.wait_ge(mT_ps, u + 1)
                    if any_yet(16 * u):
                        dve.wait_ge(nmax_stored, 16 * u)
                    nc.vector.tensor_scalar(nmax[:, 0, :], m, -1.0, None, ALU.mult).then_inc(nmax_step, 1)
                    dve.wait_ge(nmax_step, 4 * u + 1)
                    nc.vector.scalar_tensor_tensor(out=nrest[:, :], in0=m, scalar=-1.0, in1=nmax[:, 0, :],
                                                   op0=ALU.mult, op1=ALU.subtract).then_inc(nmax_step, 1)
                elif part == 1:
                    dve.wait_ge(nmax_step, 4 * u + 2)
                    nc.vector.tensor_copy(nmax[:, 1, :], nrest[:, :]).then_inc(nmax_step, 1)
                else:
                    dve.wait_ge(nmax_step, 4 * u + 3)
                    nc.vector.tensor_tensor(nmax[:, 2, :], nrest[:, :], nmax[:, 1, :],
                                            ALU.subtract).then_inc(nmax_step, 1)

            def norm_stats(s, src, i):
                for t in (2 * i, 2 * i + 1):
                    last = nc.vector.bn_stats(stats[:, s, t, :], src[:, t, :])
                if i == 3:
                    last.then_inc(c_step if s else a_step, 1)

            def norm_mean_var(b, s):
                step, mod = (c_step, mod_c) if s else (a_step, mod_a)
                dve.wait_ge(step, 3 * b + 1)
                if any_yet(4 * b):
                    dve.wait_ge(cT_ev if s else aT_ev, 4 * b)
                stand_alone(dve)
                for t in range(NT):
                    nc.vector.bn_aggr(mean_var[:, s, t, :], stats[:, s, t, :])
                nc.vector.tensor_copy(mod[:, :, :], mod_cols[:, b, :, :]).then_inc(step, 1)

            def norm_add_eps(b, s):
                step = c_step if s else a_step
                dve.wait_ge(step, 3 * b + 2)
                nc.vector.tensor_scalar(rstd[:, s, :], mean_var[:, s, :, 1], EPS, None, ALU.add).then_inc(step, 1)

            def normalise(b, s, src, i):
                dve.wait_ge(c_rstd if s else a_rstd, b + 1)
                for t in (2 * i, 2 * i + 1):
                    last = nc.vector.tensor_scalar(xn[:, t, :], src[:, t, :], mean_var[:, s, t, 0:1],
                                                   rstd[:, s, t:t + 1], ALU.subtract, ALU.mult)
                last.then_inc(c_normed if s else a_normed, 1)

            def invert(b, g):
                u = 4 * b + g
                dve.wait_ge(den_loaded, 16 * u + 16)
                nc.vector.reciprocal(den_cols[:, g % 2, :], den_cols[:, g % 2, :]).then_inc(inverted, 1)

            def divide(b, dh):
                for s in range(2):
                    dve.wait_ge(num_moved[s], 128 * b + 128)
                    dve.wait_ge(rden_spread[s], 128 * b + 128)
                nc.vector.tensor_tensor(o_num[:, dh, :], o_num[:, dh, :], o_rden[:, dh, :],
                                        ALU.mult).then_inc(divided, 1)

            def add_to_residual(bank, ps_sem, at, i, done):
                if any_yet(at):
                    dve.wait_ge(ps_sem, at)
                r = xres[:, 2 * i:2 * i + 2, :]
                nc.vector.tensor_tensor(r, bank.rearrange("p (t d) -> p t d", t=2), r,
                                        ALU.add).then_inc(done, 1)

            def attention_residual(b, i):
                dve.wait_ge(c_loaded, 48 * b + 48)
                add_to_residual(stage_c_bank(b, i), wo_ps, 4 * b + i + 1, i, x1_done)

            def feed_forward_residual(b, i):
                dve.wait_ge(biased, 8 * b + 2 * i + 2)
                add_to_residual(stage_c_bank(b, i), ff_ps, 4 * b + i + 1, i, ff_done)

            def row(b, first, last, two_more):
                for n in range(STEPS):
                    ahead = (n + AHEAD) // UNIT < 4 or not last
                    if n - 1 in MT_AT and (n - 1 != MT_AT[3] or not last):
                        g = MT_AT.index(n - 1) + 1
                        split_maxima(b + g // 4, g % 4, 0)
                    if not first:
                        if n - 1 in WO_AT:
                            attention_residual(b - 1, WO_AT.index(n - 1))
                        if n - 1 in FF_AT:
                            feed_forward_residual(b - 1, FF_AT.index(n - 1))
                    if ahead:
                        row_max(b, n, 0)
                        row_max(b, n, 1)
                    if n - 1 in MT_AT and (n - 1 != MT_AT[3] or not last):
                        g = MT_AT.index(n - 1) + 1
                        split_maxima(b + g // 4, g % 4, 1)
                    if ahead:
                        row_max(b, n, 2)
                        row_max(b, n, 3)
                    if n in (21, 33, 45):
                        invert(b, n // UNIT - 1)
                    if n == 5 and not first:
                        invert(b - 1, 3)
                    if n % UNIT == 5 and (n < 36 or not last):
                        g = n // UNIT + 1
                        join_maxima(b + g // 4, g % 4)
                    if n - 1 in MT_AT and (n - 1 != MT_AT[3] or not last):
                        g = MT_AT.index(n - 1) + 1
                        split_maxima(b + g // 4, g % 4, 2)
                    if two_more:
                        if n in STATS_A_AT:
                            if n == STATS_A_AT[0]:
                                dve.wait_ge(x_loaded, 16 * b + 48)
                            norm_stats(0, xn, STATS_A_AT.index(n))
                        if n == 37:
                            norm_mean_var(b + 2, 0)
                            norm_add_eps(b + 2, 0)
                        for i in range(4):
                            if n == (38, 38, 39, 42)[i]:
                                normalise(b + 2, 0, xn, i)
                    if not first:
                        if n in (10, 13):
                            divide(b - 1, (n - 10) // 3)
                        if n - 1 in WO_AT:
                            i = WO_AT.index(n - 1)
                            if any_yet(4 * b - 4 + i + 1):
                                dve.wait_ge(x1_done, 4 * b - 4 + i + 1)
                            norm_stats(1, xres, i)
                        if n == 19:
                            norm_mean_var(b - 1, 1)
                            norm_add_eps(b - 1, 1)
                        if n in (20, 21, 23, 24):
                            if not last:
                                dve.wait_ge(aT_ps, 4 * b + 8)
                            normalise(b - 1, 1, xres, (20, 21, 23, 24).index(n))

            dve.wait_ge(cexp_done, 1)
            nc.vector.tensor_scalar(c_exp[:, :, :], c_exp[:, :, :], 1.0, None, ALU.add).then_inc(silu_step, 1)
            dve.wait_ge(silu_step, 1)
            nc.vector.reciprocal(c_exp[:, :, :], c_exp[:, :, :]).then_inc(silu_step, 1)
            dve.wait_ge(silu_step, 2)
            nc.vector.tensor_tensor(c_sb[:, :, :], c_sb[:, :, :], c_exp[:, :, :], ALU.mult).then_inc(silu_step, 1)
            dve.wait_ge(x_loaded, 16)
            for i in range(4):
                norm_stats(0, xn, i)
            dve.wait_ge(mod_ps, 8)
            for i in range(4):
                src = ps_misc[:, B * DH * i:B * DH * (i + 1)].rearrange("p (h b) -> p b h", h=DH)
                last = nc.vector.tensor_scalar(mod_cols[:, :, i, :], src, float(i % 2), None, ALU.add)
            last.then_inc(mod_ev, 1)
            dve.wait_ge(mod_ev, 1)
            norm_mean_var(0, 0)
            norm_add_eps(0, 0)
            for i in range(4):
                normalise(0, 0, xn, i)
            dve.wait_ge(mod_ps, 10)
            g_ps = ps_out[0:B, :]
            nc.vector.tensor_scalar(g_pos, g_ps, 0.25, None, ALU.max).then_inc(gate_step, 1)
            nc.vector.tensor_scalar(g_neg, g_ps, -0.25, None, ALU.min).then_inc(gate_step, 1)
            dve.wait_ge(gate_step, 2)
            nc.vector.scalar_tensor_tensor(out=g_pos, in0=g_ps, scalar=0.0, in1=g_pos,
                                           op0=ALU.is_ge, op1=ALU.mult).then_inc(gate_step, 1)
            nc.vector.scalar_tensor_tensor(out=g_neg, in0=g_ps, scalar=0.0, in1=g_neg,
                                           op0=ALU.is_lt, op1=ALU.mult).then_inc(gate_step, 1)
            dve.wait_ge(gate_step, 4)
            nc.vector.tensor_tensor(g_pos, g_pos, g_neg, ALU.add).then_inc(gate_step, 1)
            dve.wait_ge(b_loaded, 32)
            dve.wait_ge(consts_ready, 2)

            def weigh_by_bias(g):
                dve.wait_ge(w12_loaded[g % 2], 32 * (g // 2 + 1))
                acc = bias_sums[:, g % 2, :]
                nc.vector.tensor_scalar(acc, w12[:, g % 2, 1, 0, :], b1_sb[:, g, 0:1], None,
                                        ALU.mult).then_inc(bias_summed, 1)
                for kt in range(1, KT):
                    dve.wait_ge(bias_summed, KT * g + kt)
                    nc.vector.scalar_tensor_tensor(out=acc, in0=w12[:, g % 2, 1, kt, :], scalar=b1_sb[:, g, kt:kt + 1],
                                                   in1=acc, op0=ALU.mult, op1=ALU.add).then_inc(bias_summed, 1)

            def bias_product(g):
                dve.wait_ge(w12_ps, 3 * g + 3)
                if any_yet(64 * (g // 2)):
                    dve.wait_ge(w12_stored[g % 2], 64 * (g // 2))
                nc.vector.tensor_tensor(bias_cols[:, g % 2, :], ps_exp[:, 2, 0:DH], b2_sb[:, g, :],
                                        ALU.add).then_inc(bias_ev, 1)

            weigh_by_bias(0)
            weigh_by_bias(1)
            for i in range(8):
                dve.wait_ge(qk_mid, i + 1)
                nc.vector.tensor_tensor(parts[:, i % 4, 2, :], rest[:, i % 2, :], parts[:, i % 4, 1, :],
                                        ALU.subtract).then_inc(qk_low, 1)
            bias_product(0)
            for n in range(AHEAD):
                for h in range(4):
                    row_max(0, n - AHEAD, h)
                if n % 2 == 0 and n < 2 * G - 2:
                    bias_product(1 + n // 2)
                if n % 2 == 1 and (n + 3) // 2 < G:
                    weigh_by_bias((n + 3) // 2)
                if n == UNIT - 1:
                    join_maxima(0, 0)
                if n == UNIT + 2:
                    for part in range(3):
                        split_maxima(0, 0, part)
                if n == 4:
                    dve.wait_ge(x_loaded, 32)
                if 4 <= n < 8:
                    norm_stats(0, xn, n - 4)
                if n == 8:
                    norm_mean_var(1, 0)
                    norm_add_eps(1, 0)
                if 9 <= n < 13:
                    normalise(1, 0, xn, n - 9)
            row(0, True, False, True)
            with dve.Fori(1, B - 2) as b:
                row(b, False, False, True)
            row(B - 2, False, False, False)
            row(B - 1, False, True, False)
            invert(B - 1, 3)
            divide(B - 1, 0)
            divide(B - 1, 1)
            for i in range(4):
                attention_residual(B - 1, i)
                if any_yet(4 * (B - 1) + i + 1):
                    dve.wait_ge(x1_done, 4 * (B - 1) + i + 1)
                norm_stats(1, xres, i)
            norm_mean_var(B - 1, 1)
            norm_add_eps(B - 1, 1)
            for i in range(4):
                normalise(B - 1, 1, xres, i)
            for i in range(4):
                feed_forward_residual(B - 1, i)

        @block.gpsimd
        def _(pool):
            def mask(b, n):
                pool.wait_ge(exp_done, 192 * b + 4 * n + 4)
                stand_alone(pool)
                v = probs[:, n % RING, :, 0:P]
                nc.gpsimd.affine_select(out=v, in_=v, compare_op=ALU.is_ge, fill=0.0, base=0,
                                        pattern=[[0, 4], [1, P]], channel_multiplier=-1).then_inc(masked, 1)

            def copy_values(b, g):
                u = 4 * b + g
                pool.wait_ge(v_ev, 4 * b + 4)
                if any_yet(12 * (u - 1)):
                    pool.wait_ge(pv_done, 12 * (u - 1))
                stand_alone(pool)
                nc.gpsimd.tensor_copy(v_ones[:, g % 2, :, :, 0:16],
                                      v_row[:, :, 64 * g:64 * g + 64].rearrange("p t (h d) -> p t h d", h=4)
                                      ).then_inc(v_copied, 1)

            def inverse_root(b, s):
                pool.wait_ge(c_step if s else a_step, 3 * b + 3)
                nc.gpsimd.tensor_tensor(rstd[:, s, :], rstd[:, s, :], exponent[:, :],
                                        ALU.pow).then_inc(c_rstd if s else a_rstd, 1)

            def rest_of_high(b, i):
                pool.wait_ge(qk_hi, 8 * b + i + 1)
                nc.gpsimd.tensor_tensor(rest[:, i % 2, :], rest[:, i % 2, :], parts[:, i % 4, 0, :],
                                        ALU.subtract).then_inc(qk_rest, 1)

            def low_part(b, i):
                pool.wait_ge(qk_mid, 8 * b + i + 1)
                nc.gpsimd.tensor_tensor(parts[:, i % 4, 2, :], rest[:, i % 2, :], parts[:, i % 4, 1, :],
                                        ALU.subtract).then_inc(qk_low, 1)

            def gate_weights(b, i):
                w, dh = i // 2, i % 2
                pool.wait_ge(c_loaded, 48 * b + 48)
                if any_yet(4 * b):
                    pool.wait_ge(wo_ps, 4 * b)
                src, dst = ((wo_sb, wo_gated), (ff_gated, ff_gated))[w]
                nc.gpsimd.tensor_tensor(dst[:, dh, :], src[:, dh, :], gates[:, D * w:D * w + D],
                                        ALU.mult).then_inc(gated, 1)

            def gate_bias(b):
                pool.wait_ge(gated, 4 * b + 4)
                nc.gpsimd.tensor_tensor(bias_halves, bias_halves,
                                        gates[:, D:2 * D].rearrange("q (h p) -> q h p", h=DH),
                                        ALU.mult).then_inc(bias_gated, 1)

            def add_bias(b, i):
                pool.wait_ge(bias_gated, b + 1)
                pool.wait_ge(c_normed, 4 * b + i + 1)
                for t in (2 * i, 2 * i + 1):
                    r = xres[:, t, :].rearrange("q (h p) -> q h p", h=DH)
                    nc.gpsimd.tensor_tensor(r, r, bias_halves,
                                            ALU.add).then_inc(biased, 1)

            def row(b, first, last, two_more):
                for n in range(STEPS):
                    if not last and n in QK_REST_AT:
                        rest_of_high(b + 1, QK_REST_AT.index(n))
                    if exp_step(n % UNIT)[3]:
                        mask(b, n)
                    if not last and n - 1 in QK_MID_AT:
                        low_part(b + 1, QK_MID_AT.index(n - 1))
                    if n == 37 and two_more:
                        inverse_root(b + 2, 0)
                    if not first:
                        if 8 <= n < 12:
                            gate_weights(b - 1, n - 8)
                        if n == 17:
                            gate_bias(b - 1)
                        if n == 19:
                            inverse_root(b - 1, 1)
                        if 23 <= n < 27:
                            add_bias(b - 1, n - 23)
                    if n % UNIT == 6 and (n < 36 or not last):
                        g = n // UNIT + 1
                        copy_values(b + g // 4, g % 4)

            bias_gated = sem("bias_gated")
            nc.gpsimd.memset(exponent[:, :], -0.5).then_inc(const_step, 1)
            nc.gpsimd.memset(ident[:, :], 0.0).then_inc(const_step, 1)
            nc.gpsimd.memset(causal[:, :], 0.0).then_inc(const_step, 1)
            pool.wait_ge(const_step, 3)
            nc.gpsimd.affine_select(out=ident[:, :], in_=ident[:, :], compare_op=ALU.not_equal, fill=1.0, base=0,
                                    pattern=[[-1, P]], channel_multiplier=1).then_inc(consts_ready, 1)
            nc.gpsimd.affine_select(out=causal[:, 384:512], in_=causal[:, 384:512], compare_op=ALU.is_ge,
                                    fill=-1.0e30, base=0, pattern=[[-1, P]],
                                    channel_multiplier=1).then_inc(consts_ready, 1)
            pool.wait_ge(consts_ready, 2)
            nc.gpsimd.memset(k_stack[96:99, :, :, :], 1.0).then_inc(ones_ready, 1)
            pool.wait_ge(ones_ready, 1)
            for s in range(2):
                nc.gpsimd.memset(v_ones[:, s, :, :, 16:32], 1.0).then_inc(ones_ready, 1)

            def load_w12(g):
                if any_yet(3 * (g - 1)):
                    pool.wait_ge(w12_ps, 3 * (g - 1))
                for m, w in enumerate((w1, w2)):
                    pool.dma_start(w12[:, g % 2, m], w[g].rearrange("(k p) n -> p k n", p=P)
                                   ).then_inc(w12_loaded[g % 2], 16)

            def store_product(g):
                pool.wait_ge(w12_ev, 2 * g + 2)
                pool.wait_ge(bias_ev, g + 1)
                for b in (2 * g, 2 * g + 1):
                    pool.dma_start(ff_dram[b], ff_out[:, g % 2]).then_inc(w12_stored[g % 2], 16)
                    pool.dma_start(gate_dram[b, 2 * D:3 * D].rearrange("(p h) -> p h", p=P), bias_cols[:, g % 2, :]
                                   ).then_inc(w12_stored[g % 2], 16)

            load_w12(0)
            load_w12(1)
            inverse_root(0, 0)
            for i in range(8):
                rest_of_high(0, i)
            load_w12(2)
            store_product(0)
            for g in range(1, G):
                if g + 2 < G:
                    load_w12(g + 2)
                store_product(g)
                if g == 4:
                    inverse_root(1, 0)
            copy_values(0, 0)
            row(0, True, False, True)
            with pool.Fori(1, B - 2) as b:
                row(b, False, False, True)
            row(B - 2, False, False, False)
            row(B - 1, False, True, False)
            for i in range(4):
                gate_weights(B - 1, i)
            gate_bias(B - 1)
            inverse_root(B - 1, 1)
            for i in range(4):
                add_bias(B - 1, i)


def kernel(L0_attn_x, L0_attn_WQ, L0_attn_WK, L0_attn_WV, L0_attn_WO, L0_ffn_W1, L0_ffn_b1, L0_ffn_W2, L0_ffn_b2,
           L0_c, L0_wmod):
    import numpy as np
    import concourse.bacc as bacc
    from concourse.bass_utils import run_bass_kernel_spmd

    b1 = np.asarray(L0_ffn_b1)
    groups, inner = b1.shape
    laid_out = {
        "x": np.asarray(L0_attn_x),
        "wq": np.asarray(L0_attn_WQ).T,
        "wk": np.asarray(L0_attn_WK).T,
        "wv": np.asarray(L0_attn_WV).T,
        "wo": np.asarray(L0_attn_WO).T,
        "w1": np.asarray(L0_ffn_W1),
        "b1": b1.reshape(groups, inner // P, P).transpose(2, 0, 1),
        "w2": np.asarray(L0_ffn_W2).transpose(0, 2, 1),
        "b2": np.asarray(L0_ffn_b2).reshape(groups, -1, P).transpose(2, 0, 1),
        "c": np.asarray(L0_c).T,
        "wmod": np.asarray(L0_wmod),
    }
    nc = bacc.Bacc("TRN2", target_bir_lowering=False, num_devices=1)
    arrays, args = {}, []
    for name, a in laid_out.items():
        a = np.ascontiguousarray(a)
        arrays[f"in_{name}"] = a
        args.append(nc.dram_tensor(f"in_{name}", a.shape, mybir.dt.from_np(a.dtype), kind="ExternalInput").ap())
    out = nc.dram_tensor("out_dram", laid_out["x"].shape, F32, kind="ExternalOutput").ap()
    adaln_block(nc, *args, out)
    result = run_bass_kernel_spmd(nc, [arrays], core_ids=[0])
    return result.results[0]["out_dram"]
```
